# Optimizing a Trainium2 kernel written in Bass

```python
import numpy as np
import jax
import jax.numpy as jnp

def _softmax(x, axis=-1):
    return jax.nn.softmax(x, axis=axis)
def _gelu(x):
    return jax.nn.gelu(x, approximate=True)
def _silu(x):
    return jax.nn.silu(x)
def _sigmoid(x):
    return jax.nn.sigmoid(x)
def _layernorm(x, axis=-1, eps=1e-5):
    m = jnp.mean(x, axis=axis, keepdims=True)
    v = jnp.var(x, axis=axis, keepdims=True)
    return (x - m) / jnp.sqrt(v + eps)
def _scatter_add(tgt, idx, src, axis=0):
    return tgt.at[idx].add(src)
def _segment_sum(src, seg, n):
    return jax.ops.segment_sum(src, seg, n)

kernel_name = 'mk_conv_seq_d2_conv_nhwc256_fdeba8'

def setup_inputs(seed: int = 0):
    np.random.seed(seed)
    _w = jnp.asarray
    def _rec_inputs():
        import jax
        import jax.numpy as jnp
        _gk = jax.random.key(seed)
        x = -0.0002091 + 1 * jax.random.normal(jax.random.fold_in(_gk, 1), (32, 56, 56, 256), jnp.float32)
        return x
    x = _rec_inputs()
    def _L0_conv_setup():
        import jax, jax.numpy as jnp
        import numpy as np
        from jax import lax
        N, H, W, C = (32, 56, 56, 256)
        K, RATE, STRIDE = (3, 2, 1)
        BN_EPS = 0.001
        DN = ('NHWC', 'HWIO', 'NHWC')
        key = jax.random.key(seed)
        ks = jax.random.split(key, 5)
        return {'x': jax.random.normal(ks[0], (N, H, W, C), jnp.float32), 'dw_kernel': jax.random.normal(ks[1], (K, K, 1, C), jnp.float32) * 0.1, 'dw_bias': jnp.zeros((C,), jnp.float32), 'pw_kernel': jax.random.normal(ks[2], (1, 1, C, C), jnp.float32) * 0.05, 'pw_bias': jnp.zeros((C,), jnp.float32), 'gamma': jnp.ones((C,), jnp.float32), 'beta': jnp.zeros((C,), jnp.float32), 'moving_mean': jax.random.normal(ks[3], (C,), jnp.float32) * 0.1, 'moving_var': jax.random.uniform(ks[4], (C,), jnp.float32, 0.5, 1.5)}
    _L0_conv_all = _L0_conv_setup()
    _L0_conv_in = {k: v for k, v in _L0_conv_all.items() if k in ('dw_kernel', 'dw_bias', 'pw_kernel', 'pw_bias', 'gamma', 'beta', 'moving_mean', 'moving_var', )}
    del _L0_conv_all

    def _L1_conv_setup():
        import jax, jax.numpy as jnp
        import numpy as np
        H, W, C, HID, K = (32, 32, 256, 512, 1)

        def spiral_indices(h, w):
            cy, cx = (h // 2, w // 2)
            seen, seq = (set(), [])

            def add(y, x):
                if 0 <= y < h and 0 <= x < w and ((y, x) not in seen):
                    seen.add((y, x))
                    seq.append((y, x))
            add(cy, cx)
            max_r = max(cy, h - 1 - cy, cx, w - 1 - cx)
            for r in range(1, max_r + 1):
                top, bot, left, right = (cy - r, cy + r, cx - r, cx + r)
                for x in range(left, right + 1):
                    add(top, x)
                for y in range(top + 1, bot + 1):
                    add(y, right)
                for x in range(right - 1, left - 1, -1):
                    add(bot, x)
                for y in range(bot - 1, top, -1):
                    add(y, left)
            if len(seq) != h * w:
                for y in range(h):
                    for x in range(w):
                        add(y, x)
            return seq

        def _static(h, w):
            path = spiral_indices(h, w)
            n = len(path)
            pidx = np.zeros(n, np.int32)
            nidx = np.zeros((n, 4), np.int32)
            nmask = np.zeros((n, 4), np.float32)
            ncnt = np.zeros(n, np.float32)
            for i, (y, x) in enumerate(path):
                pidx[i] = y * w + x
                cands = [(y - 1, x), (y + 1, x), (y, x - 1), (y, x + 1)]
                j = 0
                for yy, xx in cands:
                    if 0 <= yy < h and 0 <= xx < w:
                        nidx[i, j] = yy * w + xx
                        nmask[i, j] = 1.0
                        j += 1
                ncnt[i] = max(j, 1)
            return (jnp.asarray(pidx), jnp.asarray(nidx), jnp.asarray(nmask), jnp.asarray(ncnt))
        key = jax.random.key(seed)
        k0, k1, k2, k3 = jax.random.split(key, 4)
        B = 128
        x = jax.random.normal(k0, (B, H, W, C), dtype=jnp.float32)
        w1 = jax.random.normal(k1, (2 * C, HID), dtype=jnp.float32) * 0.05
        b1 = jnp.zeros((HID,), jnp.float32)
        w2 = jax.random.normal(k2, (HID,), dtype=jnp.float32) * 0.05
        b2 = jnp.zeros((), jnp.float32)
        w_y = jax.random.normal(k3, (C,), dtype=jnp.float32) * 0.05
        return {'x': x, 'w1': w1, 'b1': b1, 'w2': w2, 'b2': b2, 'w_y': w_y}
    _L1_conv_all = _L1_conv_setup()
    _L1_conv_in = {k: v for k, v in _L1_conv_all.items() if k in ('w1', 'b1', 'w2', 'b2', 'w_y', )}
    del _L1_conv_all

    return {
        "x": x,
        "L0_conv_dw_kernel": _L0_conv_in["dw_kernel"],
        "L0_conv_dw_bias": _L0_conv_in["dw_bias"],
        "L0_conv_pw_kernel": _L0_conv_in["pw_kernel"],
        "L0_conv_pw_bias": _L0_conv_in["pw_bias"],
        "L0_conv_gamma": _L0_conv_in["gamma"],
        "L0_conv_beta": _L0_conv_in["beta"],
        "L0_conv_moving_mean": _L0_conv_in["moving_mean"],
        "L0_conv_moving_var": _L0_conv_in["moving_var"],
        "L1_conv_w1": _L1_conv_in["w1"],
        "L1_conv_b1": _L1_conv_in["b1"],
        "L1_conv_w2": _L1_conv_in["w2"],
        "L1_conv_b2": _L1_conv_in["b2"],
        "L1_conv_w_y": _L1_conv_in["w_y"],
    }

def reference(x, L0_conv_dw_kernel, L0_conv_dw_bias, L0_conv_pw_kernel, L0_conv_pw_bias, L0_conv_gamma, L0_conv_beta, L0_conv_moving_mean, L0_conv_moving_var, L1_conv_w1, L1_conv_b1, L1_conv_w2, L1_conv_b2, L1_conv_w_y):
    import jax
    import jax.numpy as jnp
    def _L0_conv_ref(x, dw_kernel, dw_bias, pw_kernel, pw_bias, gamma, beta, moving_mean, moving_var):
        import jax, jax.numpy as jnp
        import numpy as np
        from jax import lax
        N, H, W, C = (32, 56, 56, 256)
        K, RATE, STRIDE = (3, 2, 1)
        BN_EPS = 0.001
        DN = ('NHWC', 'HWIO', 'NHWC')
        h = jax.nn.relu(x)
        h = lax.conv_general_dilated(h, dw_kernel, window_strides=(1, 1), padding='SAME', rhs_dilation=(RATE, RATE), dimension_numbers=DN, feature_group_count=C) + dw_bias
        h = lax.conv_general_dilated(h, pw_kernel, window_strides=(STRIDE, STRIDE), padding='SAME', dimension_numbers=DN) + pw_bias
        inv = gamma * lax.rsqrt(moving_var + BN_EPS)
        return h * inv + (beta - moving_mean * inv)

    def _L1_conv_ref(x, w1, b1, w2, b2, w_y):
        import jax, jax.numpy as jnp
        import numpy as np
        H, W, C, HID, K = (32, 32, 256, 512, 1)

        def spiral_indices(h, w):
            cy, cx = (h // 2, w // 2)
            seen, seq = (set(), [])

            def add(y, x):
                if 0 <= y < h and 0 <= x < w and ((y, x) not in seen):
                    seen.add((y, x))
                    seq.append((y, x))
            add(cy, cx)
            max_r = max(cy, h - 1 - cy, cx, w - 1 - cx)
            for r in range(1, max_r + 1):
                top, bot, left, right = (cy - r, cy + r, cx - r, cx + r)
                for x in range(left, right + 1):
                    add(top, x)
                for y in range(top + 1, bot + 1):
                    add(y, right)
                for x in range(right - 1, left - 1, -1):
                    add(bot, x)
                for y in range(bot - 1, top, -1):
                    add(y, left)
            if len(seq) != h * w:
                for y in range(h):
                    for x in range(w):
                        add(y, x)
            return seq

        def _static(h, w):
            path = spiral_indices(h, w)
            n = len(path)
            pidx = np.zeros(n, np.int32)
            nidx = np.zeros((n, 4), np.int32)
            nmask = np.zeros((n, 4), np.float32)
            ncnt = np.zeros(n, np.float32)
            for i, (y, x) in enumerate(path):
                pidx[i] = y * w + x
                cands = [(y - 1, x), (y + 1, x), (y, x - 1), (y, x + 1)]
                j = 0
                for yy, xx in cands:
                    if 0 <= yy < h and 0 <= xx < w:
                        nidx[i, j] = yy * w + xx
                        nmask[i, j] = 1.0
                        j += 1
                ncnt[i] = max(j, 1)
            return (jnp.asarray(pidx), jnp.asarray(nidx), jnp.asarray(nmask), jnp.asarray(ncnt))
        B, h, w, c = x.shape
        pidx, nidx, nmask, ncnt = _static(h, w)
        g = x.reshape(B, h * w, c)

        def step(g, inp):
            ci, ni, nm, nc = inp
            local = g[:, ci, :]
            nb = g[:, ni, :]
            neigh = (nb * nm[None, :, None]).sum(axis=1) / nc
            u = jnp.concatenate([local, neigh], axis=-1)
            y_sc = jnp.tanh(u @ w1 + b1) @ w2 + b2
            g = g.at[:, ci, :].set(local + y_sc[:, None] * w_y[None, :])
            return (g, None)
        for _ in range(K):
            g, _ = jax.lax.scan(step, g, (pidx, nidx, nmask, ncnt))
        return g.reshape(B, h, w, c)

    def _gn(v, G=32, eps=1e-5):
        B_, H_, W_, C_ = v.shape
        g = v.reshape(B_, H_, W_, G, C_ // G)
        m = jnp.mean(g, axis=(1, 2, 4), keepdims=True)
        s = jnp.var(g, axis=(1, 2, 4), keepdims=True)
        return ((g - m) / jnp.sqrt(s + eps)).reshape(v.shape)

    def _ln_c(v, eps=1e-6):
        m = jnp.mean(v, axis=-1, keepdims=True)
        s = jnp.var(v, axis=-1, keepdims=True)
        return (v - m) / jnp.sqrt(s + eps)

    def _ln_t(v, eps=1e-5):
        m = jnp.mean(v, axis=-1, keepdims=True)
        s = jnp.var(v, axis=-1, keepdims=True)
        return (v - m) / jnp.sqrt(s + eps)

    def _to_tokens(v):
        B_, H_, W_, C_ = v.shape
        return v.reshape(B_, H_ * W_, C_)
    def _from_tokens(t, like):
        return t.reshape(like.shape)

    x = _L0_conv_ref(x, L0_conv_dw_kernel, L0_conv_dw_bias, L0_conv_pw_kernel, L0_conv_pw_bias, L0_conv_gamma, L0_conv_beta, L0_conv_moving_mean, L0_conv_moving_var)
    x = _L1_conv_ref(x, L1_conv_w1, L1_conv_b1, L1_conv_w2, L1_conv_b2, L1_conv_w_y)
    return x


_drawn_inputs = setup_inputs


def setup_inputs(seed=0):
    import zlib

    import numpy as np

    out = dict(_drawn_inputs(seed))
    spreads = {'L0_conv_dw_bias': (0.0, 0.1),
     'L0_conv_pw_bias': (0.0, 0.1),
     'L0_conv_gamma': (1.0, 0.2),
     'L0_conv_beta': (0.0, 0.1),
     'L1_conv_b1': (0.0, 0.699)}
    factors = {'L1_conv_w1': 2.738}
    for name, (base, spread) in spreads.items():
        noise = np.random.default_rng([zlib.crc32(name.encode()), seed]).standard_normal(out[name].shape)
        drawn = base * np.exp(spread * noise) if base else spread * noise
        out[name] = jnp.asarray(drawn.astype(out[name].dtype))
    for name, factor in factors.items():
        out[name] = (out[name] * factor).astype(out[name].dtype)
    return out
```

```python
import numpy as np
from contextlib import ExitStack

import concourse.bass as bass
from concourse import mybir

B, H, W, C = 32, 56, 56, 256
HID = 512
P = 128
CK = C // P
NB = 16
HALVES = B // NB
WI = P // NB
T = W // WI
COLS = W * NB
PADX = 2
RROW = (W + 2 * PADX) * NB
DROW = (W + 2) * NB
R_SLOTS, D_SLOTS, X_SLOTS, N_SLOTS, O_SLOTS = 8, 4, 2, 2, 2
UNROLL = 8
LAST_STEP = H + 4
EPS = 1e-3

RINGS = H // 2
Q = P // B
GROUPS = RINGS // Q
LEVELS = 8 * RINGS
STAGE_LEVELS = LEVELS // GROUPS
BODY_LEVELS = 4
TILES = 1 + sum(STAGE_LEVELS * (GROUPS - s) for s in range(GROUPS))
WIN = 13
PAD = 7
HIST = PAD + LEVELS + 1
OUT_OF_RANGE = B * H * W


def ring_point(r, i):
    if i < 0 or i >= max(1, 8 * r):
        return None
    if r == 0:
        return H // 2, W // 2
    e, k = divmod(i, 2 * r)
    y, x = ((-r, -r + k), (-r + k, r), (r, r - k), (r - k, -r))[e]
    y, x = y + H // 2, x + W // 2
    return (y, x) if 0 <= y < H and 0 <= x < W else None


def tile_sequence():
    seq = [(0, GROUPS)]
    for s in range(GROUPS):
        for level in range(STAGE_LEVELS * s, STAGE_LEVELS * (s + 1)):
            seq += [(level, g) for g in range(GROUPS - 1 - s, -1, -1)]
    return seq


def shape_tables():
    where = {ring_point(r, i): (r, i) for r in range(RINGS + 1) for i in range(max(1, 8 * r))
             if ring_point(r, i) is not None}
    assert len(where) == H * W
    load_row = np.zeros((1, TILES * Q), np.int32)
    store_row = np.full((P, TILES), OUT_OF_RANGE, np.int32)
    coef = np.zeros((P, TILES * WIN), np.float32)
    wrap = np.zeros((P, LEVELS // BODY_LEVELS), np.float32)
    img = np.arange(B)
    for c, (level, g) in enumerate(tile_sequence()):
        for q in range(Q):
            r = RINGS - Q + 1 - Q * g + q
            rows = slice(B * q, B * (q + 1))
            at = ring_point(r, level) if r >= 0 else None
            if at is not None:
                load_row[0, c * Q + q] = ((at[0] * WI + at[1] % WI) * B) * T + at[1] // WI
                store_row[rows, c] = (img * H + at[0]) * W + at[1]
            t = level + 1
            at = ring_point(r, t) if r >= 1 and g < GROUPS else None
            if at is None:
                continue
            y, x = at
            near = [where[p] for p in ((y - 1, x), (y + 1, x), (y, x - 1), (y, x + 1)) if p in where]
            before = [p for p in near if p < (r, t)]
            for r2, i2 in before:
                if t == 8 * r - 1 and i2 == 0:
                    assert before.count((r, 0)) == 1 and before.count((r - 1, 0)) == 1
                    assert level % BODY_LEVELS == 2 and g == GROUPS - 1 - level // STAGE_LEVELS
                    wrap[rows, level // BODY_LEVELS] = 1.0 / len(near)
                    continue
                d = t - i2
                assert (r2 == r and d == 1) or (r2 == r - 1 and 1 <= d <= 7)
                col = WIN - 2 if r2 == r else WIN - 1 - 2 * (d - 1)
                coef[rows, c * WIN + col] = 1.0 / len(near)
    side = np.zeros((P, 4), np.float32)
    wi = np.arange(P) // NB
    for j, (edge, inner) in enumerate(((0, 4), (WI - 1, 4), (0, 3), (WI - 1, 3))):
        side[:, j] = 1.0 / np.where(wi == edge, inner - 1, inner)
    return load_row, store_row, coef, wrap, side


def build(nc, x, dwk, dwb, pwk, pwb, gamma, beta, mmean, mvar, w1, b1, w2, b2, wy,
          load_row, store_row, coef, wrap, side, scratch, out):
    f32, bf16, i32 = mybir.dt.float32, mybir.dt.bfloat16, mybir.dt.int32
    ALU = mybir.AluOpType
    ACT = mybir.ActivationFunctionType
    ctx = ExitStack()
    with ctx:
        def sb(name, shape, dt=f32):
            return ctx.enter_context(nc.sbuf_tensor(name, shape, dt))

        def sem(name):
            return ctx.enter_context(nc.semaphore(name))

        x_tok = sb("x_tok", [P, X_SLOTS, T * C])
        relu_rows = sb("relu_rows", [P, R_SLOTS, CK, RROW])
        dw_rows = sb("dw_rows", [P, D_SLOTS, CK, DROW])
        nsum = sb("nsum", [P, N_SLOTS, CK, COLS])
        gn_out = sb("gn_out", [P, O_SLOTS, T, 2 * C])
        ident = sb("ident", [P, P])
        pw = sb("pw", [P, CK, C])
        taps = sb("taps", [P, CK, 9])
        diag = sb("diag", [P, CK, 3, P])
        w1_g = sb("w1_g", [P, CK, HID])
        w1_n = sb("w1_n", [P, CK, HID])
        v_row = sb("v_row", [P, HID])
        w2_row = sb("w2_row", [P, HID])
        wy_row = sb("wy_row", [P, C])
        b2_col = sb("b2_col", [P, 1])
        side_sb = sb("side_sb", [P, 4])
        bias_rows = sb("bias_rows", [P, C + HID], bf16)
        pick = sb("pick", [P, P], bf16)
        store_idx = sb("store_idx", [P, TILES], i32)
        s_col = sb("s_col", [P, GROUPS])
        y_col = sb("y_col", [P, 2])
        wrap_tmp = sb("wrap_tmp", [P, 1])
        win_tmp = sb("win_tmp", [P, WIN])
        wrap_sb = sb("wrap_sb", [P, LEVELS // BODY_LEVELS])
        idx_col = sb("idx_col", [P, 4], i32)
        rr = relu_rows[:, :, :, :].rearrange("p a b c -> p (a b c)")
        coef_sb = rr[:, 0:TILES * WIN]
        hist = rr[:, TILES * WIN:TILES * WIN + GROUPS * HIST * 2].rearrange("p (g n) -> p g n", g=GROUPS)
        assert TILES * WIN + GROUPS * HIST * 2 <= R_SLOTS * CK * RROW
        dd = dw_rows[:, :, :, :].rearrange("p a b c -> p (a b c)")
        row_sb = dd[0:1, 0:TILES * Q].bitcast(i32)
        oo = gn_out[:, :, :, :].rearrange("p a b c -> p (a b c)")

        def part(n, k, size):
            at = part.at
            part.at += k * size
            return oo[:, at:at + k * size].rearrange("p (k n) -> p k n", k=k)
        part.at = 0
        x_tile = part("x_tile", 4, 2 * C)
        u_t = part("u_t", 2, 2 * C)
        pre_s = part("pre_s", 2, HID)
        th = part("th", 2, HID)
        o_tile = part("o_tile", 4, C)
        prod = part("prod", 1, HID)
        assert part.at <= O_SLOTS * T * 2 * C
        su = gn_out[:, :, :, :].rearrange("p a b c -> p (a b c)")
        gam, bet, mme, mva, pwb_r, inv, cst, t0, t1 = (su[:, C * i:C * (i + 1)] for i in range(9))
        o = 9 * C
        w1b = su[:, o:o + CK * HID].rearrange("p (k n) -> p k n", k=CK); o += CK * HID
        pw_t = su[:, o:o + CK * C].rearrange("p (k n) -> p k n", k=CK); o += CK * C
        dwb_b = su[:, o:o + CK * P].rearrange("p (k n) -> p k n", k=CK); o += CK * P
        cst_b = su[:, o:o + CK * P].rearrange("p (k n) -> p k n", k=CK); o += CK * P
        wy_b = su[:, o:o + CK * P].rearrange("p (k n) -> p k n", k=CK); o += CK * P
        b1_r = su[:, o:o + HID]; o += HID
        dwb_c = su[:, o:o + CK]; o += CK
        brow = x_tok[:, 0, 0:C + HID]
        brow2 = x_tok[:, 0, C + HID:2 * (C + HID)]
        assert o <= O_SLOTS * T * 2 * C

        psum = ctx.enter_context(nc.psum_tensor("psum", [P, 8, 512], f32))
        x_ps = psum[:, 0:2, :].rearrange("p a n -> p (a n)")
        cv_ps = psum[:, 2:4, :]
        CH = COLS // 2

        x_in = [sem(f"x_in{i}") for i in range(X_SLOTS)]
        wts_in = sem("wts_in")
        setup_pe, setup_v, setup_a, setup_p = sem("setup_pe"), sem("setup_v"), sem("setup_a"), sem("setup_p")
        x_transposed = sem("x_transposed")
        row_ready = sem("row_ready")
        centre_ready = sem("centre_ready")
        centre_read = sem("centre_read")
        conv_step = sem("conv_step")
        dw_ready = sem("dw_ready")
        nsum_ready = sem("nsum_ready")
        gn_ready = sem("gn_ready")
        gn_copied = sem("gn_copied")
        stored = [sem(f"stored{i}") for i in range(O_SLOTS)]
        tabs_in = sem("tabs_in")
        hist_zero = sem("hist_zero")
        tile_in = [sem(f"tile_in{i}") for i in range(4)]
        u_ready = sem("u_ready")
        ut_ready = sem("ut_ready")
        pre_ready = sem("pre_ready")
        pres_ready = sem("pres_ready")
        th_ready = sem("th_ready")
        y_ready = sem("y_ready")
        hist_ready = sem("hist_ready")
        s_ready = sem("s_ready")
        wrap_step = sem("wrap_step")
        out_ready = sem("out_ready")
        idx_ready = sem("idx_ready")
        out_stored = sem("out_stored")
        pool_gate = sem("pool_gate")
        tile_out = [sem(f"tile_out{i}") for i in range(4)]

        x_v = x.rearrange("b h (w t) c -> h b w (t c)", t=T)
        sc_rows = scratch.rearrange("h w b t n -> (h w b t) n")
        sc_v = scratch.rearrange("h w (b a) t n -> h (w b) a (t n)", a=HALVES)
        out_rows = out.rearrange("b h w c -> (b h w) c")

        N_W = 17

        def row_steps(eng, step):
            with eng.Fori(0, HALVES) as h:
                for k in range(UNROLL):
                    step(h, k, k)
                with eng.Fori(1, H // UNROLL) as j:
                    for k in range(UNROLL):
                        step(h, j * UNROLL + k, UNROLL + k)
                for k in range(H, LAST_STEP + 1):
                    step(h, k, k)

        def levels(eng, tile):
            c0 = 1
            for s in range(GROUPS):
                n = GROUPS - s
                iters = STAGE_LEVELS // BODY_LEVELS
                with eng.Fori(0, iters) as it:
                    for l in range(BODY_LEVELS):
                        for j in range(n):
                            k = l * n + j
                            tile(c0 + k + it * (BODY_LEVELS * n), c0 + k,
                                 (c0 + k) // 4 + it * n, s * STAGE_LEVELS + it * BODY_LEVELS + l,
                                 n, j, l, s * iters + it)
                c0 += STAGE_LEVELS * n

        block = ctx.enter_context(nc.Block())

        @block.sync
        def _(sp):
            bc = lambda a, n: a.partition_broadcast(P)
            loads = [
                (gam, bc(gamma, C)), (bet, bc(beta, C)), (mme, bc(mmean, C)), (mva, bc(mvar, C)),
                (pwb_r, bc(pwb, C)), (wy_row[:, :], bc(wy, C)), (w2_row[:, :], bc(w2, HID)),
                (b1_r, bc(b1, HID)), (b2_col[:, :], bc(b2, 1)),
                (pw[:, :, :], pwk.rearrange("a b (k p) n -> p (a b k) n", p=P)),
                (w1_g[:, :, :], w1[0:C, :].rearrange("(k p) n -> p k n", p=P)),
                (w1b, w1[C:2 * C, :].rearrange("(k p) n -> p k n", p=P)),
                (side_sb[:, :], side), (store_idx[:, :], store_row), (wrap_sb[:, :], wrap),
            ]
            for dst, src in loads:
                sp.dma_start(dst, src).then_inc(wts_in, 16)
            for k in range(CK):
                sp.dma_start(taps[:, k, :], dwk.rearrange("a b o (k p) -> k p (a b o)", p=P)[k],
                             allow_slow_non_contiguous=True).then_inc(wts_in, 16)
            sp.dma_start(dwb_c, dwb.rearrange("(k p) -> p k", p=P),
                         allow_slow_non_contiguous=True).then_inc(wts_in, 16)
            sp.wait_ge(setup_pe, 7)

            def step(h, k, kk):
                if kk < H:
                    sp.wait_ge(x_transposed, 1 + h * (2 * H) + (2 * k - 2 if kk >= 2 else 0))
                    sp.dma_start(x_tok[:, kk % X_SLOTS, :],
                                 x_v[k, bass.ds(h, NB, HALVES), :, :]).then_inc(x_in[kk % X_SLOTS], 16)
                if kk >= 7:
                    store(h, k - 7, kk - 7)

            def store(h, z, zz):
                sp.wait_ge(gn_copied, 1 + h * (4 * H) + 4 * z + 4)
                sp.dma_start(sc_v[z, :, h, :], gn_out[:, zz % O_SLOTS, :, :].rearrange("p t n -> p (t n)")
                             ).then_inc(stored[zz % O_SLOTS], 16)

            with sp.Fori(0, HALVES) as h:
                for k in range(UNROLL):
                    step(h, k, k)
                with sp.Fori(1, H // UNROLL) as j:
                    for k in range(UNROLL):
                        step(h, j * UNROLL + k, UNROLL + k)
                for k in range(H, LAST_STEP + 3):
                    step(h, k, k)

            for i in range(O_SLOTS):
                sp.wait_ge(stored[i], 16 + 16 * HALVES * (H // O_SLOTS))
            sp.dma_start(row_sb, load_row).then_inc(tabs_in, 16)
            sp.dma_start(coef_sb, coef).then_inc(tabs_in, 16)
            sp.wait_ge(tabs_in, 32)
            regs = [sp.alloc_register(f"row{q}") for q in range(Q)]

            def load(c, cc, per_slot, *_):
                sp.load(regs, row_sb[0:1, bass.ds(c * Q, Q)])
                sp.wait_ge(out_ready, c + 1)
                for q in range(Q):
                    row = sp.snap(regs[q], min_val=0, max_val=(H * WI - 1) * B * T + T - 1)
                    sp.dma_start(x_tile[B * q:B * (q + 1), cc % 4, :],
                                 sc_rows[bass.ds(row, B, T), :]).then_inc(tile_in[cc % 4], 16)

            load(0, 0, 0)
            levels(sp, load)

        @block.gpsimd
        def _(pool):
            pool.sem_inc(out_stored, 4)
            pool.memset(ident[:, :], 0.0).then_inc(setup_p, 1)
            pool.memset(pick[:, :], 0.0)
            pool.memset(bias_rows[:, :], 0.0)
            pool.memset(relu_rows[:, :, :, :], 0.0)
            pool.memset(dw_rows[:, :, :, :], 0.0)
            pool.memset(s_col[:, :], 0.0).then_inc(setup_p, 1)
            pool.wait_ge(setup_p, 2)
            pool.affine_select(out=ident[:, :], in_=ident[:, :], compare_op=ALU.not_equal, fill=1.0,
                               base=0, pattern=[[-1, P]], channel_multiplier=1).then_inc(setup_p, 1)
            for i in range(O_SLOTS):
                pool.wait_ge(stored[i], 16 + 16 * HALVES * (H // O_SLOTS))
            pool.memset(hist, 0.0).then_inc(hist_zero, 1)
            pool.wait_ge(wts_in, 16 * (N_W + 1))

            def store(c, cc, per_slot, *_):
                pool.wait_ge(out_stored, c + 1)
                pool.sem_inc(pool_gate, 1)
                pool.tensor_copy(idx_col[:, cc % 4:cc % 4 + 1], store_idx[:, bass.ds(c, 1)]).then_inc(idx_ready, 1)
                pool.wait_ge(idx_ready, c + 1)
                pool.sem_inc(pool_gate, 1)
                pool.wait_ge(out_ready, 4 + c + 1)
                pool.sem_inc(pool_gate, 1)
                pool.indirect_dma_start(out_rows, bass.IndirectOffsetOnAxis(idx_col[:, cc % 4:cc % 4 + 1], 0),
                                        o_tile[:, cc % 4, :], None, bounds_check=OUT_OF_RANGE - 1,
                                        oob_is_err=False).then_inc(tile_out[cc % 4], 16)
                if cc:
                    before = per_slot if cc % 4 else per_slot - 1
                    pool.wait_ge(tile_out[(cc - 1) % 4], 16 * (before + 1))
                    pool.sem_inc(out_stored, 1)

            store(0, 0, 0)
            levels(pool, store)
            for i in range(4):
                pool.wait_ge(tile_out[i], 16 * len(range(i, TILES, 4)))

        @block.scalar
        def _(act):
            act.wait_ge(setup_v, 1)
            act.activation(t1, t0, ACT.Sqrt).then_inc(setup_a, 1)
            act.sem_inc(row_ready, 1)
            act.sem_inc(ut_ready, 2)
            act.sem_inc(th_ready, 2)
            act.sem_inc(gn_copied, 1)
            for i in range(O_SLOTS):
                act.sem_inc(stored[i], 16)
            act.wait_ge(setup_p, 3)
            act.wait_ge(setup_pe, 7)
            act.wait_ge(setup_v, SETUP_V)

            def step(h, k, kk):
                if kk < H:
                    for c in range(CK):
                        act.wait_ge(x_transposed, 1 + h * (2 * H) + 2 * k + c + 1)
                        if c == 0:
                            act.wait_ge(dw_ready, 1 + h * H + (k - 5 if kk >= 6 else 0))
                        act.activation(relu_rows[:, kk % R_SLOTS, c, PADX * NB:PADX * NB + COLS].rearrange(
                                           "p (w t b) -> p t b w", t=T, b=NB),
                                       x_ps[:, 0:COLS].rearrange("p (t b w) -> p t b w", b=NB, w=WI),
                                       ACT.Relu).then_inc(row_ready, 1)
                z, zz = k - 5, kk - 5
                if 0 <= zz < H:
                    edge = zz in (0, H - 1)
                    for i in range(4):
                        tiles = range(2 * i, min(2 * i + 2, T))
                        act.wait_ge(gn_ready, 1 + h * (4 * H) + 4 * z + i + 1)
                        if i == 0:
                            act.wait_ge(stored[zz % O_SLOTS], 16 + h * (8 * H) + 8 * (z - zz % 2))
                        bank = 4 + 2 * (i % 2)
                        act.activation(gn_out[:, zz % O_SLOTS, tiles[0]:tiles[-1] + 1, 0:C],
                                       psum[:, bank:bank + len(tiles), 0:C], ACT.Copy)
                        inner = [t for t in tiles if t not in (0, T - 1)]
                        for t in tiles:
                            if t in (0, T - 1):
                                col = (2 if edge else 0) + (t == T - 1)
                                last = act.activation(gn_out[:, zz % O_SLOTS, t, C:2 * C],
                                                      psum[:, bank + t % 2, C:2 * C], ACT.Copy,
                                                      scale=side_sb[:, col:col + 1])
                        if inner:
                            b0 = bank + inner[0] % 2
                            last = act.activation(gn_out[:, zz % O_SLOTS, inner[0]:inner[-1] + 1, C:2 * C],
                                                  psum[:, b0:b0 + len(inner), C:2 * C], ACT.Copy,
                                                  scale=1.0 / (3 if edge else 4))
                        last.then_inc(gn_copied, 1)

            row_steps(act, step)

            def copy_u(c, cc):
                act.wait_ge(u_ready, c + 1)
                act.wait_ge(pre_ready, c + 1)
                act.activation(u_t[:, cc % 2, :], psum[:, cc % 2, :], ACT.Copy).then_inc(ut_ready, 1)

            def tile(c, cc, *_, ahead=2):
                if ahead:
                    copy_u(c + ahead, cc + ahead)
                act.wait_ge(pres_ready, 4 + c + 1)
                act.wait_ge(y_ready, c + 1)
                act.activation(th[:, cc % 2, :], pre_s[:, cc % 2, :], ACT.Tanh).then_inc(th_ready, 1)

            copy_u(0, 0)
            copy_u(1, 1)
            tile(0, 0)
            c0 = 1
            for s in range(GROUPS):
                n = GROUPS - s
                per, iters = BODY_LEVELS * n, STAGE_LEVELS // BODY_LEVELS
                last_stage = s == GROUPS - 1
                with act.Fori(0, iters - last_stage) as it:
                    for k in range(per):
                        tile(c0 + k + it * per, c0 + k)
                if last_stage:
                    for k in range(TILES - per, TILES):
                        tile(k, k, ahead=2 if k + 2 < TILES else 0)
                c0 += STAGE_LEVELS * n

        @block.vector
        def _(dve):
            done = [0]

            def link(ins):
                done[0] += 1
                ins.then_inc(setup_v, 1)
                dve.wait_ge(setup_v, done[0])

            dve.wait_ge(wts_in, 16 * (N_W + 1))
            link(dve.tensor_scalar(t0, mva, EPS, None, ALU.add))
            dve.wait_ge(setup_a, 1)
            link(dve.reciprocal(inv, t1))
            link(dve.tensor_tensor(inv, inv, t0, ALU.mult))
            link(dve.tensor_tensor(t1, t1, inv, ALU.add))
            link(dve.tensor_scalar(t1, t1, 0.5, None, ALU.mult))
            link(dve.reciprocal(inv, t1))
            link(dve.tensor_tensor(inv, inv, gam, ALU.mult))
            for k in range(CK):
                link(dve.tensor_tensor(pw[:, k, :], pw[:, k, :], inv, ALU.mult))
            link(dve.tensor_tensor(cst, pwb_r, mme, ALU.subtract))
            link(dve.tensor_tensor(cst, cst, inv, ALU.mult))
            link(dve.tensor_tensor(cst, cst, bet, ALU.add))
            link(dve.memset(dwb_b, 0.0))
            for k in range(CK):
                link(dve.tensor_scalar(dwb_b[:, k, :], dwb_b[:, k, :], dwb_c[:, k:k + 1], None, ALU.add))
            dve.wait_ge(setup_p, 3)
            for p in (0, 32, 64):
                link(dve.memset(pick[p:p + 1, :], 1.0))
            for k in range(CK):
                for j in range(3):
                    link(dve.tensor_scalar(diag[:, k, j, :], ident[:, :], taps[:, k, 3 + j:4 + j], None, ALU.mult))
            dve.wait_ge(setup_pe, 1)
            link(dve.tensor_tensor(cst, cst, psum[:, 0, 0:C], ALU.add))
            assert done[0] == SETUP_CST
            dve.wait_ge(setup_pe, 2)
            link(dve.tensor_copy(pw_t[:, 0, :], psum[:, 1, 0:C]))
            link(dve.tensor_copy(pw_t[:, 1, :], psum[:, 1, C:2 * C]))
            link(dve.tensor_copy(cst_b, psum[:, 2, 0:C].rearrange("p (k n) -> p k n", k=CK)))
            link(dve.tensor_copy(wy_b, psum[:, 2, C:2 * C].rearrange("p (k n) -> p k n", k=CK)))
            assert done[0] == SETUP_T
            dve.wait_ge(setup_pe, 3)
            for k in range(CK):
                link(dve.tensor_copy(w1_n[:, k, :], psum[:, 4 + k, :]))
            dve.wait_ge(setup_pe, 4)
            link(dve.tensor_copy(v_row[:, :], psum[:, 6, :]))
            dve.wait_ge(setup_pe, 5)
            link(dve.tensor_copy(brow[:, 0:C], cst))
            link(dve.tensor_tensor(brow[:, C:C + HID], b1_r, psum[:, 7, :], ALU.add))
            for i, p in enumerate((0, 32, 64)):
                link(dve.tensor_copy(bias_rows[p:p + 1, :], brow[p:p + 1, :]))
                if i < 2:
                    for p2 in (0, 32, 64)[i + 1:]:
                        link(dve.tensor_copy(bias_rows[p2:p2 + 1, :], brow[p2:p2 + 1, :]))
                        link(dve.tensor_tensor(brow2[p2:p2 + 1, :], brow[p2:p2 + 1, :],
                                               bias_rows[p2:p2 + 1, :], ALU.subtract))
                        link(dve.tensor_copy(brow[p2:p2 + 1, :], brow2[p2:p2 + 1, :]))
            assert done[0] == SETUP_V
            dve.sem_inc(dw_ready, 1)
            dve.sem_inc(centre_read, 1)
            dve.sem_inc(pres_ready, 4)
            dve.sem_inc(y_ready, 2)
            dve.sem_inc(s_ready, GROUPS)
            dve.sem_inc(out_ready, 4)

            ops = {"n": 0}
            HALF_OPS = half_ops()

            def chain(ins):
                ops["n"] = ops["n"] + 1
                ins.then_inc(conv_step, 1)
                return ops["n"]

            def step(h, k, kk):
                y, yy = k - 3, kk - 3
                if 0 <= yy < H:
                    kys = [ky for ky in (0, 2) if 0 <= yy + 2 * (ky - 1) < H]
                    for c in range(CK):
                        dst = dw_rows[:, yy % D_SLOTS, c, NB:NB + COLS]

                        def src(ky, kx):
                            r = (yy + 2 * (ky - 1)) % R_SLOTS
                            return relu_rows[:, r, c, 2 * kx * NB:2 * kx * NB + COLS]

                        rows = [(ky, kx) for ky in kys for kx in range(3)]
                        for i, (ky, kx) in enumerate(rows):
                            w = taps[:, c, 3 * ky + kx:3 * ky + kx + 1]
                            if i == 0:
                                dve.wait_ge(centre_ready, h * (2 * H) + 2 * y + c + 1)
                                if c == 0:
                                    dve.wait_ge(row_ready, 1 + h * (2 * H) + (2 * y + 6 if yy + 2 < H else 2 * H))
                                    dve.wait_ge(gn_ready, 1 + h * (4 * H) + (4 * (y - 3) if yy >= 4 else 0))
                                n = chain(dve.scalar_tensor_tensor(
                                    out=dst.rearrange("p (a n) -> p a n", a=2),
                                    in0=src(ky, kx).rearrange("p (a n) -> p a n", a=2), scalar=w,
                                    in1=cv_ps[:, :, 0:CH], op0=ALU.mult, op1=ALU.add))
                                dve.wait_ge(conv_step, n)
                                dve.sem_inc(centre_read, 1)
                            else:
                                n = chain(dve.scalar_tensor_tensor(out=dst, in0=src(ky, kx), scalar=w, in1=dst,
                                                                   op0=ALU.mult, op1=ALU.add))
                                dve.wait_ge(conv_step, n)
                    dve.sem_inc(dw_ready, 1)
                z, zz = k - 4, kk - 4
                if 0 <= zz < H:
                    dst = nsum[:, zz % N_SLOTS, :, :]
                    dve.wait_ge(gn_ready, 1 + h * (4 * H) + (4 * (z - 1) if zz >= 2 else 0))
                    mid = dw_rows[:, zz % D_SLOTS, :, :]
                    last = dve.tensor_tensor(dst, mid[:, :, 0:COLS], mid[:, :, 2 * NB:2 * NB + COLS], ALU.add)
                    for dz in (-1, 1):
                        if 0 <= zz + dz < H:
                            dve.wait_ge(conv_step, chain(last))
                            last = dve.tensor_tensor(dst, dst, dw_rows[:, (zz + dz) % D_SLOTS, :, NB:NB + COLS], ALU.add)
                    dve.wait_ge(conv_step, chain(last))
                    dve.sem_inc(nsum_ready, 1)

            with dve.Fori(0, HALVES) as h:
                ops["n"] = h * HALF_OPS
                for k in range(UNROLL):
                    step(h, k, k)
                first = half_ops(UNROLL)
                body = half_ops(2 * UNROLL) - first
                with dve.Fori(1, H // UNROLL) as j:
                    ops["n"] = h * HALF_OPS + (first - body) + j * body
                    for k in range(UNROLL):
                        step(h, j * UNROLL + k, UNROLL + k)
                ops["n"] = h * HALF_OPS + half_ops(H)
                for k in range(H, LAST_STEP + 1):
                    step(h, k, k)

            dve.wait_ge(tabs_in, 32)
            dve.wait_ge(hist_zero, 1)

            def add_s(c, cc, n, j):
                dve.wait_ge(pre_ready, 2 + c + 1)
                dve.wait_ge(th_ready, c + 1)
                dve.wait_ge(s_ready, GROUPS + c - n)
                g = n - 1 - j
                dve.scalar_tensor_tensor(out=pre_s[:, cc % 2, :], in0=v_row[:, :], scalar=s_col[:, g:g + 1],
                                         in1=psum[:, 4 + cc % 4, :], op0=ALU.mult,
                                         op1=ALU.add).then_inc(pres_ready, 1)

            def finish(c, cc, per_slot, level, n, j, l, body):
                g = n - 1 - j if n else GROUPS
                y = y_col[:, cc % 2:cc % 2 + 1]
                dve.wait_ge(th_ready, 2 + c + 1)
                dve.tensor_tensor_reduce(out=prod[:, 0, :], in0=th[:, cc % 2, :], in1=w2_row[:, :], scale=1.0,
                                         scalar=b2_col[:, 0:1], op0=ALU.mult, op1=ALU.add,
                                         accum_out=y).then_inc(y_ready, 1)
                dve.wait_ge(y_ready, 2 + c + 1)
                own = (level + PAD) * 2
                inner = own + 1
                if n:
                    dve.tensor_copy(hist[:, g, bass.ds(own, 1)], y)
                    for q in range(1, Q):
                        last = dve.tensor_copy(hist[B * q:B * (q + 1), g, bass.ds(inner, 1)],
                                               y_col[B * (q - 1):B * q, cc % 2:cc % 2 + 1])
                if g > 0:
                    last = dve.tensor_copy(hist[0:B, g - 1, bass.ds(inner, 1)],
                                           y_col[B * (Q - 1):P, cc % 2:cc % 2 + 1])
                last.then_inc(hist_ready, 1)
                if n:
                    dve.wait_ge(hist_ready, c + 1)
                    dve.scalar_tensor_tensor(out=win_tmp[:, :], in0=hist[:, g, bass.ds(level * 2 + 3, WIN)],
                                             scalar=1.0, in1=coef_sb[:, bass.ds(c * WIN, WIN)], op0=ALU.mult,
                                             op1=ALU.mult, accum_out=s_col[:, g:g + 1]).then_inc(s_ready, 1)
                    if l == 2 and j == 0:
                        dve.wait_ge(s_ready, GROUPS + c)
                        dve.tensor_tensor(wrap_tmp[:, :], hist[:, g, 2 * PAD:2 * PAD + 1],
                                          hist[:, g, 2 * PAD + 1:2 * PAD + 2], ALU.add).then_inc(wrap_step, 1)
                        dve.wait_ge(wrap_step, 2 * body + 1)
                        dve.scalar_tensor_tensor(out=s_col[:, g:g + 1], in0=wrap_tmp[:, :],
                                                 scalar=wrap_sb[:, bass.ds(body, 1)], in1=s_col[:, g:g + 1],
                                                 op0=ALU.mult, op1=ALU.add).then_inc(wrap_step, 1)
                        dve.wait_ge(wrap_step, 2 * body + 2)
                dve.wait_ge(out_stored, c + 1)
                dve.scalar_tensor_tensor(out=o_tile[:, cc % 4, :], in0=wy_row[:, :], scalar=y,
                                         in1=x_tile[:, cc % 4, 0:C], op0=ALU.mult,
                                         op1=ALU.add).then_inc(out_ready, 1)

            add_s(0, 0, 1, 0)
            finish(0, 0, 0, 0, 0, 0, 0, 0)
            waiting = []

            def tile(*a):
                c, cc, per_slot, level, n, j, l, body = a
                add_s(c, cc, n, j)
                if j:
                    finish(*waiting.pop())
                waiting.append(a)
                if j == n - 1:
                    finish(*waiting.pop())

            levels(dve, tile)

        @block.tensor
        def _(pe):
            pe.wait_ge(setup_v, SETUP_DIAG)
            for k in range(CK):
                last = pe.matmul(psum[:, 0, 0:C], dwb_b[:, k, :], pw[:, k, :], start=k == 0, stop=k == CK - 1)
            last.then_inc(setup_pe, 1)
            pe.wait_ge(setup_v, SETUP_CST)
            for k in range(CK):
                for m in range(CK):
                    pe.transpose(psum[:, 1, C * m + P * k:C * m + P * (k + 1)], pw[:, k, P * m:P * (m + 1)], ident[:, :])
            for k in range(CK):
                pe.transpose(psum[:, 2, P * k:P * (k + 1)], cst[:, P * k:P * (k + 1)], ident[:, :])
                last = pe.transpose(psum[:, 2, C + P * k:C + P * (k + 1)], wy_row[:, P * k:P * (k + 1)], ident[:, :])
            last.then_inc(setup_pe, 1)
            pe.wait_ge(setup_v, SETUP_T)
            for k in range(CK):
                for m in range(CK):
                    last = pe.matmul(psum[:, 4 + k, :], pw_t[:, m, P * k:P * (k + 1)], w1b[:, m, :],
                                     start=m == 0, stop=m == CK - 1)
            last.then_inc(setup_pe, 1)
            for bank, lhs in ((6, wy_b), (7, cst_b)):
                for m in range(CK):
                    last = pe.matmul(psum[:, bank, :], lhs[:, m, :], w1b[:, m, :], start=m == 0, stop=m == CK - 1)
                last.then_inc(setup_pe, 1)
            pe.wait_ge(setup_v, SETUP_V)
            pe.sem_inc(setup_pe, 2)
            pe.sem_inc(x_transposed, 1)
            pe.sem_inc(gn_ready, 1)
            pe.sem_inc(pre_ready, 2)

            def transpose_row(h, k, kk, c):
                if c == 0:
                    pe.wait_ge(x_in[kk % X_SLOTS], h * (8 * H) + 8 * (k - kk % 2) + 16)
                pe.wait_ge(row_ready, 1 + h * (2 * H) + 2 * k + c)
                for t in range(T):
                    last = pe.transpose(x_ps[:, P * t:P * (t + 1)],
                                        x_tok[:, kk % X_SLOTS, t * C + c * P:t * C + (c + 1) * P], ident[:, :])
                last.then_inc(x_transposed, 1)

            def centre_taps(h, y, yy, c):
                pe.wait_ge(row_ready, 1 + h * (2 * H) + 2 * y + 2)
                pe.wait_ge(centre_read, 1 + h * (2 * H) + 2 * y + c)
                for half in range(2):
                    for kx in range(3):
                        at = 2 * kx * NB + half * CH
                        last = pe.matmul(cv_ps[:, half, 0:CH], diag[:, c, kx, :],
                                         relu_rows[:, yy % R_SLOTS, c, at:at + CH], start=kx == 0, stop=kx == 2)
                last.then_inc(centre_ready, 1)

            def to_tokens(h, z, zz, i):
                if i == 0:
                    pe.wait_ge(nsum_ready, h * H + z + 1)
                pe.wait_ge(gn_copied, 1 + h * (4 * H) + (4 * z + i - 1 if zz or i else 0))
                for t in range(2 * i, min(2 * i + 2, T)):
                    bank = 4 + 2 * (i % 2) + t % 2
                    pe.matmul(psum[:, bank, 0:C], pick[:, :], bias_rows[:, 0:C], start=True, stop=False)
                    for c in range(CK):
                        pe.matmul(psum[:, bank, 0:C], dw_rows[:, zz % D_SLOTS, c, NB + P * t:NB + P * (t + 1)],
                                  pw[:, c, :], start=False, stop=c == CK - 1)
                    for c in range(CK):
                        last = pe.transpose(psum[:, bank, C + P * c:C + P * (c + 1)],
                                            nsum[:, zz % N_SLOTS, c, P * t:P * (t + 1)], ident[:, :])
                last.then_inc(gn_ready, 1)

            def step(h, k, kk):
                y, yy, z, zz = k - 3, kk - 3, k - 5, kk - 5
                for c in range(CK):
                    if 0 <= yy < H:
                        centre_taps(h, y, yy, c)
                    if kk < H:
                        transpose_row(h, k, kk, c)
                    if 0 <= zz < H:
                        to_tokens(h, z, zz, 2 * c)
                        to_tokens(h, z, zz, 2 * c + 1)

            row_steps(pe, step)

            def transpose_tile(c, cc, per_slot):
                pe.wait_ge(tile_in[cc % 4], 16 * Q * (per_slot + 1))
                pe.wait_ge(ut_ready, c + 1)
                for k in range(4):
                    last = pe.transpose(psum[:, cc % 2, P * k:P * (k + 1)], x_tile[:, cc % 4, P * k:P * (k + 1)], ident[:, :])
                last.then_inc(u_ready, 1)

            def hidden(c, cc):
                pe.wait_ge(ut_ready, 2 + c + 1)
                pe.wait_ge(pres_ready, c + 1)
                bank = psum[:, 4 + cc % 4, :]
                pe.matmul(bank, pick[:, :], bias_rows[:, C:C + HID], start=True, stop=False)
                for k in range(4):
                    w = (w1_g if k < CK else w1_n)[:, k % CK, :]
                    last = pe.matmul(bank, u_t[:, cc % 2, P * k:P * (k + 1)], w, start=False, stop=k == 3)
                last.then_inc(pre_ready, 1)

            transpose_tile(0, 0, 0)
            transpose_tile(1, 1, 0)
            hidden(0, 0)
            c0 = 1
            for s in range(GROUPS):
                n = GROUPS - s
                per, iters = BODY_LEVELS * n, STAGE_LEVELS // BODY_LEVELS
                last_stage = s == GROUPS - 1
                with pe.Fori(0, iters - last_stage) as it:
                    for k in range(per):
                        cc = c0 + k
                        transpose_tile(cc + 1 + it * per, cc + 1, (cc + 1) // 4 + it * n)
                        hidden(cc + it * per, cc)
                if last_stage:
                    for cc in range(TILES - per, TILES):
                        if cc + 1 < TILES:
                            transpose_tile(cc + 1, cc + 1, (cc + 1) // 4)
                        hidden(cc, cc)
                c0 += STAGE_LEVELS * n


SETUP_DIAG = 1 + 6 + CK + 3 + 1 + CK + 3
SETUP_CST = SETUP_DIAG + 3 * CK + 1
SETUP_T = SETUP_CST + 4
SETUP_V = SETUP_T + CK + 1 + 2 + (1 + 6) + (1 + 3) + 1


def half_ops(steps=LAST_STEP + 1):
    n = 0
    for k in range(steps):
        if 0 <= k - 3 < H:
            n += CK * 3 * sum(0 <= k - 3 + d < H for d in (-2, 2))
        if 0 <= k - 4 < H:
            n += 1 + sum(0 <= k - 4 + d < H for d in (-1, 1))
    return n


_INPUTS = ["x", "L0_conv_dw_kernel", "L0_conv_dw_bias", "L0_conv_pw_kernel", "L0_conv_pw_bias",
           "L0_conv_gamma", "L0_conv_beta", "L0_conv_moving_mean", "L0_conv_moving_var",
           "L1_conv_w1", "L1_conv_b1", "L1_conv_w2", "L1_conv_b2", "L1_conv_w_y"]


def kernel(**inputs):
    import concourse.bacc as bacc
    from concourse.bass_utils import run_bass_kernel_spmd

    nc = bacc.Bacc("TRN2", target_bir_lowering=False, num_devices=1)
    arrays, aps = {}, []
    named = [(n, np.ascontiguousarray(inputs[n])) for n in _INPUTS]
    named = [(n, a.reshape(1) if a.ndim == 0 else a) for n, a in named]
    named += list(zip(("load_row", "store_row", "coef", "wrap", "side"), shape_tables()))
    for n, a in named:
        arrays[n] = a
        aps.append(nc.dram_tensor(n, a.shape, mybir.dt.from_np(a.dtype), kind="ExternalInput").ap())
    scratch = nc.dram_tensor("scratch", (H, WI, B, T, 2 * C), mybir.dt.float32, kind="Internal").ap()
    out = nc.dram_tensor("out", (B, H, W, C), mybir.dt.float32, kind="ExternalOutput").ap()
    build(nc, *aps, scratch, out)
    r = run_bass_kernel_spmd(nc, [arrays], core_ids=[0])
    return r.results[0]["out"]
```

```python
import numpy as np
from contextlib import ExitStack

import concourse.bass as bass
from concourse import mybir

B, H, W, C = 32, 56, 56, 256
HID = 512
P = 128
CK = C // P
NB = 16
HALVES = B // NB
WI = P // NB
T = W // WI
COLS = W * NB
PADX = 2
RROW = (W + 2 * PADX) * NB
DROW = (W + 2) * NB
R_SLOTS, D_SLOTS, X_SLOTS, N_SLOTS, O_SLOTS = 8, 4, 2, 2, 2
UNROLL = 8
LAST_STEP = H + 5
EPS = 1e-3

RINGS = H // 2
Q = P // B
GROUPS = RINGS // Q
LEVELS = 8 * RINGS
STAGE_LEVELS = LEVELS // GROUPS
BODY_LEVELS = 8
U_SLOTS, TILE_SLOTS, OUT_SLOTS, AHEAD = 4, 8, 4, 2
TILES = 1 + sum(STAGE_LEVELS * (GROUPS - s) for s in range(GROUPS))
WRAP_LEVEL = 6
WIN = 13
PAD = 7
HIST = PAD + LEVELS + 1
OUT_OF_RANGE = B * H * W


def ring_point(r, i):
    if i < 0 or i >= max(1, 8 * r):
        return None
    if r == 0:
        return H // 2, W // 2
    e, k = divmod(i, 2 * r)
    y, x = ((-r, -r + k), (-r + k, r), (r, r - k), (r - k, -r))[e]
    y, x = y + H // 2, x + W // 2
    return (y, x) if 0 <= y < H and 0 <= x < W else None


def tile_sequence():
    seq = [(0, GROUPS)]
    for s in range(GROUPS):
        for level in range(STAGE_LEVELS * s, STAGE_LEVELS * (s + 1)):
            seq += [(level, g) for g in range(GROUPS - 1 - s, -1, -1)]
    return seq


def shape_tables():
    where = {ring_point(r, i): (r, i) for r in range(RINGS + 1) for i in range(max(1, 8 * r))
             if ring_point(r, i) is not None}
    assert len(where) == H * W
    load_row = np.zeros((1, TILES * Q), np.int32)
    store_row = np.full((P, TILES), OUT_OF_RANGE, np.int32)
    coef = np.zeros((P, TILES * WIN), np.float32)
    wrap = np.zeros((P, LEVELS // BODY_LEVELS), np.float32)
    img = np.arange(B)
    for c, (level, g) in enumerate(tile_sequence()):
        for q in range(Q):
            r = RINGS - Q + 1 - Q * g + q
            rows = slice(B * q, B * (q + 1))
            at = ring_point(r, level) if r >= 0 else None
            if at is not None:
                load_row[0, c * Q + q] = ((at[0] * WI + at[1] % WI) * B) * T + at[1] // WI
                store_row[rows, c] = (img * H + at[0]) * W + at[1]
            t = level + 1
            at = ring_point(r, t) if r >= 1 and g < GROUPS else None
            if at is None:
                continue
            y, x = at
            near = [where[p] for p in ((y - 1, x), (y + 1, x), (y, x - 1), (y, x + 1)) if p in where]
            before = [p for p in near if p < (r, t)]
            for r2, i2 in before:
                if t == 8 * r - 1 and i2 == 0:
                    assert before.count((r, 0)) == 1 and before.count((r - 1, 0)) == 1
                    assert level % BODY_LEVELS == WRAP_LEVEL and g == GROUPS - 1 - level // STAGE_LEVELS
                    wrap[rows, level // BODY_LEVELS] = 1.0 / len(near)
                    continue
                d = t - i2
                assert (r2 == r and d == 1) or (r2 == r - 1 and 1 <= d <= 7)
                col = WIN - 2 if r2 == r else WIN - 1 - 2 * (d - 1)
                n = GROUPS - level // STAGE_LEVELS
                coef[rows, (c - n + 1 + 2 * g) * WIN + col] = 1.0 / len(near)
    side = np.zeros((P, 4), np.float32)
    wi = np.arange(P) // NB
    for j, (edge, inner) in enumerate(((0, 4), (WI - 1, 4), (0, 3), (WI - 1, 3))):
        side[:, j] = 1.0 / np.where(wi == edge, inner - 1, inner)
    return load_row, store_row, coef, wrap, side


def build(nc, x, dwk, dwb, pwk, pwb, gamma, beta, mmean, mvar, w1, b1, w2, b2, wy,
          load_row, store_row, coef, wrap, side, scratch, out):
    f32, f32r = mybir.dt.float32, mybir.dt.float32r
    bf16, i32 = mybir.dt.bfloat16, mybir.dt.int32
    ALU = mybir.AluOpType
    ACT = mybir.ActivationFunctionType
    AX = mybir.AxisListType
    ctx = ExitStack()
    with ctx:
        def sb(name, shape, dt=f32):
            return ctx.enter_context(nc.sbuf_tensor(name, shape, dt))

        def sem(name):
            return ctx.enter_context(nc.semaphore(name))

        x_tok = sb("x_tok", [P, X_SLOTS, T * C])
        relu_rows = sb("relu_rows", [P, R_SLOTS, CK, RROW])
        dw_rows = sb("dw_rows", [P, D_SLOTS, CK, DROW])
        nsum = sb("nsum", [P, N_SLOTS, CK, COLS])
        gn_out = sb("gn_out", [P, O_SLOTS, T, 2 * C])
        ident = sb("ident", [P, P])
        pw = sb("pw", [P, CK, C])
        taps = sb("taps", [P, CK, 9])
        diag = sb("diag", [P, CK, 3, P])
        w1_hi = sb("w1_hi", [P, 2 * CK, HID], f32r)
        w1_lo = sb("w1_lo", [P, 2 * CK, HID], f32r)
        u_hi = sb("u_hi", [P, U_SLOTS, 2 * C], f32r)
        u_lo = sb("u_lo", [P, U_SLOTS, 2 * C], f32r)
        v_row = sb("v_row", [P, HID])
        w2_row = sb("w2_row", [P, HID])
        wy_row = sb("wy_row", [P, C])
        b2_col = sb("b2_col", [P, 1])
        side_sb = sb("side_sb", [P, 4])
        bias_rows = sb("bias_rows", [P, C + HID], bf16)
        pick = sb("pick", [P, P], bf16)
        store_idx = sb("store_idx", [P, TILES], i32)
        s_col = sb("s_col", [P, GROUPS])
        y_lvl = sb("y_lvl", [P, 2, GROUPS])
        wrap_tmp = sb("wrap_tmp", [P, 1])
        win_tmp = sb("win_tmp", [P, GROUPS, WIN])
        wrap_sb = sb("wrap_sb", [P, LEVELS // BODY_LEVELS])
        idx_col = sb("idx_col", [P, OUT_SLOTS], i32)
        rr = relu_rows[:, :, :, :].rearrange("p a b c -> p (a b c)")
        coef_sb = rr[:, 0:TILES * WIN]
        hist = rr[:, TILES * WIN:TILES * WIN + GROUPS * HIST * 2].rearrange("p (g n) -> p g n", g=GROUPS)
        assert TILES * WIN + GROUPS * HIST * 2 <= R_SLOTS * CK * RROW
        dd = dw_rows[:, :, :, :].rearrange("p a b c -> p (a b c)")
        row_sb = dd[0:1, 0:TILES * Q].bitcast(i32)
        oo = gn_out[:, :, :, :].rearrange("p a b c -> p (a b c)")

        def part(n, k, size):
            at = part.at
            part.at += k * size
            return oo[:, at:at + k * size].rearrange("p (k n) -> p k n", k=k)
        part.at = 0
        x_tile = part("x_tile", TILE_SLOTS, 2 * C)
        pre_s = part("pre_s", 2, HID)
        th = part("th", 2, HID)
        o_tile = part("o_tile", OUT_SLOTS, C)
        prod = x_tok[:, 0, 0:HID]
        assert part.at <= O_SLOTS * T * 2 * C
        su = gn_out[:, :, :, :].rearrange("p a b c -> p (a b c)")
        gam, bet, mme, mva, pwb_r, inv, cst, t0, t1 = (su[:, C * i:C * (i + 1)] for i in range(9))
        o = 9 * C
        w1b = su[:, o:o + CK * HID].rearrange("p (k n) -> p k n", k=CK); o += CK * HID
        pw_t = su[:, o:o + CK * C].rearrange("p (k n) -> p k n", k=CK); o += CK * C
        dwb_b = su[:, o:o + CK * P].rearrange("p (k n) -> p k n", k=CK); o += CK * P
        cst_b = su[:, o:o + CK * P].rearrange("p (k n) -> p k n", k=CK); o += CK * P
        wy_b = su[:, o:o + CK * P].rearrange("p (k n) -> p k n", k=CK); o += CK * P
        b1_r = su[:, o:o + HID]; o += HID
        dwb_c = su[:, o:o + CK]; o += CK
        w1a = su[:, o:o + CK * HID].rearrange("p (k n) -> p k n", k=CK); o += CK * HID
        brow = x_tok[:, 0, 0:C + HID]
        brow2 = x_tok[:, 0, C + HID:2 * (C + HID)]
        assert o <= O_SLOTS * T * 2 * C

        psum = ctx.enter_context(nc.psum_tensor("psum", [P, 8, 512], f32))
        x_ps = psum[:, 0:2, :].rearrange("p a n -> p (a n)")
        cv_ps = psum[:, 2:4, :]
        CH = COLS // 2

        x_in = [sem(f"x_in{i}") for i in range(X_SLOTS)]
        wts_in = sem("wts_in")
        setup_pe, setup_v, setup_a, setup_p = sem("setup_pe"), sem("setup_v"), sem("setup_a"), sem("setup_p")
        x_transposed = sem("x_transposed")
        row_ready = sem("row_ready")
        centre_ready = sem("centre_ready")
        centre_read = sem("centre_read")
        conv_step = sem("conv_step")
        dw_ready = sem("dw_ready")
        nsum_ready = sem("nsum_ready")
        gn_ready = sem("gn_ready")
        gn_copied = sem("gn_copied")
        stored = [sem(f"stored{i}") for i in range(O_SLOTS)]
        tabs_in = sem("tabs_in")
        hist_zero = sem("hist_zero")
        tile_in = [sem(f"tile_in{i}") for i in range(TILE_SLOTS)]
        u_ready = sem("u_ready")
        hi_ready = sem("hi_ready")
        lo_ready = sem("lo_ready")
        pre_ready = sem("pre_ready")
        pres_ready = sem("pres_ready")
        th_ready = sem("th_ready")
        y_ready = sem("y_ready")
        hist_ready = sem("hist_ready")
        win_ready = sem("win_ready")
        s_ready = sem("s_ready")
        wrap_step = sem("wrap_step")
        out_ready = sem("out_ready")
        idx_ready = sem("idx_ready")
        out_stored = sem("out_stored")
        pool_gate = sem("pool_gate")
        tile_out = [sem(f"tile_out{i}") for i in range(OUT_SLOTS)]

        x_v = x.rearrange("b h (w t) c -> h b w (t c)", t=T)
        sc_rows = scratch.rearrange("h w b t n -> (h w b t) n")
        sc_v = scratch.rearrange("h w (b a) t n -> h (w b) a (t n)", a=HALVES)
        out_rows = out.rearrange("b h w c -> (b h w) c")

        N_W = 17

        def row_steps(eng, step):
            with eng.Fori(0, HALVES) as h:
                for k in range(UNROLL):
                    step(h, k, k)
                with eng.Fori(1, H // UNROLL) as j:
                    for k in range(UNROLL):
                        step(h, j * UNROLL + k, UNROLL + k)
                for k in range(H, LAST_STEP + 1):
                    step(h, k, k)

        def levels(eng, tile):
            c0 = 1
            for s in range(GROUPS):
                n = GROUPS - s
                iters = STAGE_LEVELS // BODY_LEVELS

                def body(it):
                    for l in range(BODY_LEVELS):
                        for j in range(n):
                            cc = c0 + l * n + j
                            tile(cc + it * (BODY_LEVELS * n), cc, it,
                                 s * STAGE_LEVELS + it * BODY_LEVELS + l, n, j, l, s * iters + it)

                last_stage = s == GROUPS - 1
                with eng.Fori(0, iters - last_stage) as it:
                    body(it)
                if last_stage:
                    body(iters - 1)
                c0 += STAGE_LEVELS * n

        def times(cc, it, n, slots):
            return cc // slots + it * (BODY_LEVELS * n // slots)

        block = ctx.enter_context(nc.Block())

        @block.sync
        def _(sp):
            bc = lambda a, n: a.partition_broadcast(P)
            loads = [
                (gam, bc(gamma, C)), (bet, bc(beta, C)), (mme, bc(mmean, C)), (mva, bc(mvar, C)),
                (pwb_r, bc(pwb, C)), (wy_row[:, :], bc(wy, C)), (w2_row[:, :], bc(w2, HID)),
                (b1_r, bc(b1, HID)), (b2_col[:, :], bc(b2, 1)),
                (pw[:, :, :], pwk.rearrange("a b (k p) n -> p (a b k) n", p=P)),
                (w1a, w1[0:C, :].rearrange("(k p) n -> p k n", p=P)),
                (w1b, w1[C:2 * C, :].rearrange("(k p) n -> p k n", p=P)),
                (side_sb[:, :], side), (store_idx[:, :], store_row), (wrap_sb[:, :], wrap),
            ]
            for dst, src in loads:
                sp.dma_start(dst, src).then_inc(wts_in, 16)
            for k in range(CK):
                sp.dma_start(taps[:, k, :], dwk.rearrange("a b o (k p) -> k p (a b o)", p=P)[k],
                             allow_slow_non_contiguous=True).then_inc(wts_in, 16)
            sp.dma_start(dwb_c, dwb.rearrange("(k p) -> p k", p=P),
                         allow_slow_non_contiguous=True).then_inc(wts_in, 16)
            sp.wait_ge(setup_pe, 7)

            def step(h, k, kk):
                if kk < H:
                    sp.wait_ge(x_transposed, 1 + h * (2 * H) + (2 * k - 2 if kk >= 2 else 0))
                    sp.dma_start(x_tok[:, kk % X_SLOTS, :],
                                 x_v[k, bass.ds(h, NB, HALVES), :, :]).then_inc(x_in[kk % X_SLOTS], 16)
                if kk >= 8:
                    store(h, k - 8, kk - 8)

            def store(h, z, zz):
                sp.wait_ge(gn_copied, 1 + h * (4 * H) + 4 * z + 4)
                sp.dma_start(sc_v[z, :, h, :], gn_out[:, zz % O_SLOTS, :, :].rearrange("p t n -> p (t n)")
                             ).then_inc(stored[zz % O_SLOTS], 16)

            with sp.Fori(0, HALVES) as h:
                for k in range(UNROLL):
                    step(h, k, k)
                with sp.Fori(1, H // UNROLL) as j:
                    for k in range(UNROLL):
                        step(h, j * UNROLL + k, UNROLL + k)
                for k in range(H, LAST_STEP + 3):
                    step(h, k, k)

            for i in range(O_SLOTS):
                sp.wait_ge(stored[i], 16 + 16 * HALVES * (H // O_SLOTS))
            sp.dma_start(row_sb, load_row).then_inc(tabs_in, 16)
            sp.dma_start(coef_sb, coef).then_inc(tabs_in, 16)
            sp.wait_ge(tabs_in, 32)
            regs = [sp.alloc_register(f"row{q}") for q in range(Q)]

            def load(c, cc, *_):
                sp.load(regs, row_sb[0:1, bass.ds(c * Q, Q)])
                sp.wait_ge(out_ready, c + 1)
                for q in range(Q):
                    row = sp.snap(regs[q], min_val=0, max_val=(H * WI - 1) * B * T + T - 1)
                    sp.dma_start(x_tile[B * q:B * (q + 1), cc % TILE_SLOTS, :],
                                 sc_rows[bass.ds(row, B, T), :]).then_inc(tile_in[cc % TILE_SLOTS], 16)

            load(0, 0)
            levels(sp, load)

        @block.gpsimd
        def _(pool):
            pool.sem_inc(out_stored, OUT_SLOTS)
            pool.memset(ident[:, :], 0.0).then_inc(setup_p, 1)
            pool.memset(pick[:, :], 0.0)
            pool.memset(bias_rows[:, :], 0.0)
            pool.memset(relu_rows[:, :, :, :], 0.0)
            pool.memset(dw_rows[:, :, :, :], 0.0)
            pool.memset(s_col[:, :], 0.0).then_inc(setup_p, 1)
            pool.wait_ge(setup_p, 2)
            pool.affine_select(out=ident[:, :], in_=ident[:, :], compare_op=ALU.not_equal, fill=1.0,
                               base=0, pattern=[[-1, P]], channel_multiplier=1).then_inc(setup_p, 1)
            for i in range(O_SLOTS):
                pool.wait_ge(stored[i], 16 + 16 * HALVES * (H // O_SLOTS))
            pool.memset(hist, 0.0).then_inc(hist_zero, 1)
            pool.wait_ge(wts_in, 16 * (N_W + 1))

            def store(c, cc, it, level, n, *_):
                slot = cc % OUT_SLOTS
                pool.wait_ge(out_stored, c + 1)
                pool.sem_inc(pool_gate, 1)
                pool.tensor_copy(idx_col[:, slot:slot + 1], store_idx[:, bass.ds(c, 1)]).then_inc(idx_ready, 1)
                pool.wait_ge(idx_ready, c + 1)
                pool.sem_inc(pool_gate, 1)
                pool.wait_ge(out_ready, TILE_SLOTS + c + 1)
                pool.sem_inc(pool_gate, 1)
                pool.indirect_dma_start(out_rows, bass.IndirectOffsetOnAxis(idx_col[:, slot:slot + 1], 0),
                                        o_tile[:, slot, :], None, bounds_check=OUT_OF_RANGE - 1,
                                        oob_is_err=False).then_inc(tile_out[slot], 16)
                if cc:
                    pool.wait_ge(tile_out[(cc - 1) % OUT_SLOTS], 16 * (times(cc - 1, it, n, OUT_SLOTS) + 1))
                    pool.sem_inc(out_stored, 1)

            store(0, 0, 0, 0, 0)
            levels(pool, store)
            for i in range(OUT_SLOTS):
                pool.wait_ge(tile_out[i], 16 * len(range(i, TILES, OUT_SLOTS)))

        @block.scalar
        def _(act):
            act.wait_ge(setup_v, 1)
            act.activation(t1, t0, ACT.Sqrt).then_inc(setup_a, 1)
            act.sem_inc(row_ready, 1)
            act.sem_inc(th_ready, 2)
            act.sem_inc(gn_copied, 1)
            for i in range(O_SLOTS):
                act.sem_inc(stored[i], 16)
            act.wait_ge(setup_p, 3)
            act.wait_ge(setup_pe, 7)
            act.wait_ge(setup_v, SETUP_V)

            def relu(h, k, kk, c):
                act.wait_ge(x_transposed, 1 + h * (2 * H) + 2 * k + c + 1)
                if c == 0:
                    act.wait_ge(dw_ready, 1 + h * H + (k - 5 if kk >= 6 else 0))
                act.activation(relu_rows[:, kk % R_SLOTS, c, PADX * NB:PADX * NB + COLS].rearrange(
                                   "p (w t b) -> p t b w", t=T, b=NB),
                               x_ps[:, 0:COLS].rearrange("p (t b w) -> p t b w", b=NB, w=WI),
                               ACT.Relu).then_inc(row_ready, 1)

            def copy_out(h, z, zz, i):
                edge = zz in (0, H - 1)
                tiles = range(2 * i, min(2 * i + 2, T))
                act.wait_ge(gn_ready, 1 + h * (4 * H) + 4 * z + i + 1)
                if i == 0:
                    act.wait_ge(stored[zz % O_SLOTS], 16 + h * (8 * H) + 8 * (z - zz % 2))
                bank = 4 + 2 * (i % 2)
                act.activation(gn_out[:, zz % O_SLOTS, tiles[0]:tiles[-1] + 1, 0:C],
                               psum[:, bank:bank + len(tiles), 0:C], ACT.Copy)
                inner = [t for t in tiles if t not in (0, T - 1)]
                for t in tiles:
                    if t in (0, T - 1):
                        col = (2 if edge else 0) + (t == T - 1)
                        last = act.activation(gn_out[:, zz % O_SLOTS, t, C:2 * C],
                                              psum[:, bank + t % 2, C:2 * C], ACT.Copy,
                                              scale=side_sb[:, col:col + 1])
                if inner:
                    b0 = bank + inner[0] % 2
                    last = act.activation(gn_out[:, zz % O_SLOTS, inner[0]:inner[-1] + 1, C:2 * C],
                                          psum[:, b0:b0 + len(inner), C:2 * C], ACT.Copy,
                                          scale=1.0 / (3 if edge else 4))
                last.then_inc(gn_copied, 1)

            def step(h, k, kk):
                for c in range(CK):
                    if kk < H:
                        relu(h, k, kk, c)
                    if 0 <= kk - 6 < H:
                        copy_out(h, k - 6, kk - 6, 2 * c)
                        copy_out(h, k - 6, kk - 6, 2 * c + 1)

            row_steps(act, step)

            def high_part(c, cc):
                act.wait_ge(u_ready, c + 1)
                act.wait_ge(pre_ready, c + 1)
                act.activation(u_hi[:, cc % U_SLOTS, :], psum[:, cc % 4, :], ACT.Copy).then_inc(hi_ready, 1)

            def tile(c, cc, *_):
                if not isinstance(c, int) or c + AHEAD < TILES:
                    high_part(c + AHEAD, cc + AHEAD)
                act.wait_ge(pres_ready, 4 + c + 1)
                act.wait_ge(y_ready, c + 1)
                act.activation(th[:, cc % 2, :], pre_s[:, cc % 2, :], ACT.Tanh).then_inc(th_ready, 1)

            for c in range(AHEAD):
                high_part(c, c)
            tile(0, 0)
            levels(act, tile)

        @block.vector
        def _(dve):
            done = [0]

            def link(ins):
                done[0] += 1
                ins.then_inc(setup_v, 1)
                dve.wait_ge(setup_v, done[0])

            dve.wait_ge(wts_in, 16 * (N_W + 1))
            link(dve.tensor_scalar(t0, mva, EPS, None, ALU.add))
            dve.wait_ge(setup_a, 1)
            link(dve.reciprocal(inv, t1))
            link(dve.tensor_tensor(inv, inv, t0, ALU.mult))
            link(dve.tensor_tensor(t1, t1, inv, ALU.add))
            link(dve.tensor_scalar(t1, t1, 0.5, None, ALU.mult))
            link(dve.reciprocal(inv, t1))
            link(dve.tensor_tensor(inv, inv, gam, ALU.mult))
            for k in range(CK):
                link(dve.tensor_tensor(pw[:, k, :], pw[:, k, :], inv, ALU.mult))
            link(dve.tensor_tensor(cst, pwb_r, mme, ALU.subtract))
            link(dve.tensor_tensor(cst, cst, inv, ALU.mult))
            link(dve.tensor_tensor(cst, cst, bet, ALU.add))
            link(dve.memset(dwb_b, 0.0))
            for k in range(CK):
                link(dve.tensor_scalar(dwb_b[:, k, :], dwb_b[:, k, :], dwb_c[:, k:k + 1], None, ALU.add))
            dve.wait_ge(setup_p, 3)
            for p in (0, 32, 64):
                link(dve.memset(pick[p:p + 1, :], 1.0))
            for k in range(CK):
                for j in range(3):
                    link(dve.tensor_scalar(diag[:, k, j, :], ident[:, :], taps[:, k, 3 + j:4 + j], None, ALU.mult))
            dve.wait_ge(setup_pe, 1)
            link(dve.tensor_tensor(cst, cst, psum[:, 0, 0:C], ALU.add))
            assert done[0] == SETUP_CST
            dve.wait_ge(setup_pe, 2)
            link(dve.tensor_copy(pw_t[:, 0, :], psum[:, 1, 0:C]))
            link(dve.tensor_copy(pw_t[:, 1, :], psum[:, 1, C:2 * C]))
            link(dve.tensor_copy(cst_b, psum[:, 2, 0:C].rearrange("p (k n) -> p k n", k=CK)))
            link(dve.tensor_copy(wy_b, psum[:, 2, C:2 * C].rearrange("p (k n) -> p k n", k=CK)))
            assert done[0] == SETUP_T
            dve.wait_ge(setup_pe, 3)
            for k in range(2 * CK):
                w = w1a[:, k, :] if k < CK else psum[:, 2 + k, :]
                link(dve.tensor_copy(w1_hi[:, k, :], w))
                link(dve.tensor_tensor(w1_lo[:, k, :], w, w1_hi[:, k, :].bitcast(f32), ALU.subtract))
            dve.wait_ge(setup_pe, 4)
            link(dve.tensor_copy(v_row[:, :], psum[:, 6, :]))
            dve.wait_ge(setup_pe, 5)
            link(dve.tensor_copy(brow[:, 0:C], cst))
            link(dve.tensor_tensor(brow[:, C:C + HID], b1_r, psum[:, 7, :], ALU.add))
            for i, p in enumerate((0, 32, 64)):
                link(dve.tensor_copy(bias_rows[p:p + 1, :], brow[p:p + 1, :]))
                if i < 2:
                    for p2 in (0, 32, 64)[i + 1:]:
                        link(dve.tensor_copy(bias_rows[p2:p2 + 1, :], brow[p2:p2 + 1, :]))
                        link(dve.tensor_tensor(brow2[p2:p2 + 1, :], brow[p2:p2 + 1, :],
                                               bias_rows[p2:p2 + 1, :], ALU.subtract))
                        link(dve.tensor_copy(brow[p2:p2 + 1, :], brow2[p2:p2 + 1, :]))
            assert done[0] == SETUP_V
            dve.sem_inc(dw_ready, 1)
            dve.sem_inc(centre_read, 1)
            dve.sem_inc(pres_ready, 4)
            dve.sem_inc(y_ready, 2)
            dve.sem_inc(s_ready, 1)
            dve.sem_inc(lo_ready, 4)
            dve.sem_inc(out_ready, TILE_SLOTS)

            ops = {"n": 0}
            HALF_OPS = half_ops()

            def chain(ins):
                ops["n"] = ops["n"] + 1
                ins.then_inc(conv_step, 1)
                return ops["n"]

            def conv_chain(h, y, yy, c):
                dst = dw_rows[:, yy % D_SLOTS, c, NB:NB + COLS]
                steps = []
                for ky in (0, 2):
                    if not 0 <= yy + 2 * (ky - 1) < H:
                        continue
                    for kx in range(3):
                        src = relu_rows[:, (yy + 2 * (ky - 1)) % R_SLOTS, c, 2 * kx * NB:2 * kx * NB + COLS]
                        w = taps[:, c, 3 * ky + kx:3 * ky + kx + 1]
                        steps.append((src, w))

                def one(i, src, w):
                    if i == 0:
                        dve.wait_ge(centre_ready, h * (2 * H) + 2 * y + c + 1)
                        return dve.scalar_tensor_tensor(
                            out=dst.rearrange("p (a n) -> p a n", a=2),
                            in0=src.rearrange("p (a n) -> p a n", a=2), scalar=w,
                            in1=cv_ps[:, :, 0:CH], op0=ALU.mult, op1=ALU.add)
                    return dve.scalar_tensor_tensor(out=dst, in0=src, scalar=w, in1=dst, op0=ALU.mult, op1=ALU.add)

                for i, (src, w) in enumerate(steps):
                    n = chain(one(i, src, w))
                    yield
                    dve.wait_ge(conv_step, n)
                    if i == 0:
                        dve.sem_inc(centre_read, 1)

            def sum_chain(h, z, zz):
                dst = nsum[:, zz % N_SLOTS, :, :]
                dve.wait_ge(gn_ready, 1 + h * (4 * H) + (4 * (z - 1) if zz >= 2 else 0))
                mid = dw_rows[:, zz % D_SLOTS, :, :]
                n = chain(dve.tensor_tensor(dst, mid[:, :, 0:COLS], mid[:, :, 2 * NB:2 * NB + COLS], ALU.add))
                for dz in (-1, 1):
                    if 0 <= zz + dz < H:
                        yield
                        dve.wait_ge(conv_step, n)
                        n = chain(dve.tensor_tensor(dst, dst, dw_rows[:, (zz + dz) % D_SLOTS, :, NB:NB + COLS], ALU.add))
                yield
                dve.wait_ge(conv_step, n)
                dve.sem_inc(nsum_ready, 1)

            def step(h, k, kk):
                y, yy, z, zz = k - 3, kk - 3, k - 5, kk - 5
                first, second = [], []
                if 0 <= yy < H:
                    dve.wait_ge(row_ready, 1 + h * (2 * H) + (2 * y + 6 if yy + 2 < H else 2 * H))
                    dve.wait_ge(gn_ready, 1 + h * (4 * H) + (4 * (y - 3) if yy >= 4 else 0))
                    first.append(conv_chain(h, y, yy, 0))
                if 0 <= zz < H:
                    second.append(sum_chain(h, z, zz))
                elif first:
                    next(first[0])
                if 0 <= yy < H:
                    second.append(conv_chain(h, y, yy, 1))
                while first or second:
                    for queue in (first, second):
                        while queue:
                            if next(queue[0], queue) is queue:
                                queue.pop(0)
                                continue
                            break
                if 0 <= yy < H:
                    dve.sem_inc(dw_ready, 1)

            with dve.Fori(0, HALVES) as h:
                ops["n"] = h * HALF_OPS
                for k in range(UNROLL):
                    step(h, k, k)
                first = half_ops(UNROLL)
                body = half_ops(2 * UNROLL) - first
                with dve.Fori(1, H // UNROLL) as j:
                    ops["n"] = h * HALF_OPS + (first - body) + j * body
                    for k in range(UNROLL):
                        step(h, j * UNROLL + k, UNROLL + k)
                ops["n"] = h * HALF_OPS + half_ops(H)
                for k in range(H, LAST_STEP + 1):
                    step(h, k, k)

            dve.wait_ge(tabs_in, 32)
            dve.wait_ge(hist_zero, 1)

            def low_part(c, cc):
                dve.wait_ge(hi_ready, c + 1)
                slot = cc % U_SLOTS
                dve.tensor_tensor(u_lo[:, slot, :], psum[:, cc % 4, :], u_hi[:, slot, :].bitcast(f32),
                                  ALU.subtract).then_inc(lo_ready, 1)

            def add_s(c, cc, level, g):
                dve.wait_ge(pre_ready, 4 + c + 1)
                dve.wait_ge(th_ready, c + 1)
                dve.wait_ge(s_ready, level + 1)
                dve.scalar_tensor_tensor(out=pre_s[:, cc % 2, :], in0=v_row[:, :], scalar=s_col[:, g:g + 1],
                                         in1=psum[:, 4 + cc % 4, :], op0=ALU.mult,
                                         op1=ALU.add).then_inc(pres_ready, 1)

            def dot(c, cc, y):
                dve.wait_ge(th_ready, 2 + c + 1)
                dve.tensor_tensor_reduce(out=prod, in0=th[:, cc % 2, :], in1=w2_row[:, :], scale=1.0,
                                         scalar=b2_col[:, 0:1], op0=ALU.mult, op1=ALU.add,
                                         accum_out=y).then_inc(y_ready, 1)

            def finish(c, cc, y):
                dve.wait_ge(y_ready, 2 + c + 1)
                dve.wait_ge(out_stored, c + 1)
                dve.scalar_tensor_tensor(out=o_tile[:, cc % OUT_SLOTS, :], in0=wy_row[:, :], scalar=y,
                                         in1=x_tile[:, cc % TILE_SLOTS, 0:C], op0=ALU.mult,
                                         op1=ALU.add).then_inc(out_ready, 1)

            def next_s(c, level, n, l, body, ys):
                dve.wait_ge(y_ready, 2 + c + 1)
                own = (level + PAD) * 2
                dve.tensor_copy(hist[:, 0:n, bass.ds(own, 1)], ys[:, 0:n].rearrange("p (g o) -> p g o", o=1))
                for q in range(Q):
                    src = ys[B * ((q - 1) % Q):B * ((q - 1) % Q + 1), (q == 0):n]
                    if q or n > 1:
                        last = dve.tensor_copy(hist[B * q:B * (q + 1), 0:n - (q == 0), bass.ds(own + 1, 1)],
                                               src.rearrange("p (g o) -> p g o", o=1))
                last.then_inc(hist_ready, 1)
                dve.wait_ge(hist_ready, level + 2)
                first = c - (n - 1)
                dve.tensor_tensor(win_tmp[:, 0:n, :], hist[:, 0:n, bass.ds(level * 2 + 3, WIN)],
                                  coef_sb[:, bass.ds(first * WIN, n * WIN)].rearrange("p (g w) -> p g w", g=n),
                                  ALU.mult).then_inc(win_ready, 1)
                dve.wait_ge(win_ready, level + 1)
                dve.tensor_reduce(s_col[:, 0:n], win_tmp[:, 0:n, :], axis=AX.X, op=ALU.add).then_inc(s_ready, 1)
                if l == WRAP_LEVEL:
                    g = n - 1
                    dve.tensor_tensor(wrap_tmp[:, :], hist[:, g, 2 * PAD:2 * PAD + 1],
                                      hist[:, g, 2 * PAD + 1:2 * PAD + 2], ALU.add).then_inc(wrap_step, 1)
                    dve.wait_ge(s_ready, level + 2)
                    dve.wait_ge(wrap_step, 2 * body + 1)
                    dve.scalar_tensor_tensor(out=s_col[:, g:g + 1], in0=wrap_tmp[:, :],
                                             scalar=wrap_sb[:, bass.ds(body, 1)], in1=s_col[:, g:g + 1],
                                             op0=ALU.mult, op1=ALU.add).then_inc(wrap_step, 1)
                    dve.wait_ge(wrap_step, 2 * body + 2)

            def y_of(level, g):
                return y_lvl[:, level % 2, g:g + 1]

            for c in range(AHEAD):
                low_part(c, c)
            centre_y = y_of(1, 0)
            add_s(0, 0, 0, 0)
            low_part(AHEAD, AHEAD)
            dot(0, 0, centre_y)
            dve.wait_ge(y_ready, 2 + 1)
            dve.tensor_copy(hist[0:B, GROUPS - 1, 2 * PAD + 1:2 * PAD + 2],
                            y_lvl[B * (Q - 1):P, 1, 0:1]).then_inc(hist_ready, 1)
            before = [centre_y]

            def tile(c, cc, it, level, n, j, l, body):
                g = n - 1 - j
                add_s(c, cc, level, g)
                if not isinstance(c, int) or c + AHEAD < TILES:
                    low_part(c + AHEAD, cc + AHEAD)
                if j:
                    dot(c - 1, cc - 1, y_of(l, g + 1))
                finish(c - 1, cc - 1, y_of(l, g + 1) if j else y_of(l - 1, 0))
                if j == n - 1:
                    dot(c, cc, y_of(l, 0))
                    next_s(c, level, n, l, body, y_lvl[:, l % 2, 0:GROUPS])

            levels(dve, tile)
            finish(TILES - 1, TILES - 1, y_of(BODY_LEVELS - 1, 0))

        @block.tensor
        def _(pe):
            pe.wait_ge(setup_v, SETUP_DIAG)
            for k in range(CK):
                last = pe.matmul(psum[:, 0, 0:C], dwb_b[:, k, :], pw[:, k, :], start=k == 0, stop=k == CK - 1)
            last.then_inc(setup_pe, 1)
            pe.wait_ge(setup_v, SETUP_CST)
            for k in range(CK):
                for m in range(CK):
                    pe.transpose(psum[:, 1, C * m + P * k:C * m + P * (k + 1)], pw[:, k, P * m:P * (m + 1)], ident[:, :])
            for k in range(CK):
                pe.transpose(psum[:, 2, P * k:P * (k + 1)], cst[:, P * k:P * (k + 1)], ident[:, :])
                last = pe.transpose(psum[:, 2, C + P * k:C + P * (k + 1)], wy_row[:, P * k:P * (k + 1)], ident[:, :])
            last.then_inc(setup_pe, 1)
            pe.wait_ge(setup_v, SETUP_T)
            for k in range(CK):
                for m in range(CK):
                    last = pe.matmul(psum[:, 4 + k, :], pw_t[:, m, P * k:P * (k + 1)], w1b[:, m, :],
                                     start=m == 0, stop=m == CK - 1)
            last.then_inc(setup_pe, 1)
            for bank, lhs in ((6, wy_b), (7, cst_b)):
                for m in range(CK):
                    last = pe.matmul(psum[:, bank, :], lhs[:, m, :], w1b[:, m, :], start=m == 0, stop=m == CK - 1)
                last.then_inc(setup_pe, 1)
            pe.wait_ge(setup_v, SETUP_V)
            pe.sem_inc(setup_pe, 2)
            pe.sem_inc(x_transposed, 1)
            pe.sem_inc(gn_ready, 1)
            pe.sem_inc(pre_ready, 4)

            def transpose_row(h, k, kk, c):
                if c == 0:
                    pe.wait_ge(x_in[kk % X_SLOTS], h * (8 * H) + 8 * (k - kk % 2) + 16)
                pe.wait_ge(row_ready, 1 + h * (2 * H) + 2 * k + c)
                for t in range(T):
                    last = pe.transpose(x_ps[:, P * t:P * (t + 1)],
                                        x_tok[:, kk % X_SLOTS, t * C + c * P:t * C + (c + 1) * P], ident[:, :])
                last.then_inc(x_transposed, 1)

            def centre_taps(h, y, yy, c):
                pe.wait_ge(row_ready, 1 + h * (2 * H) + 2 * y + 2)
                pe.wait_ge(centre_read, 1 + h * (2 * H) + 2 * y + c)
                for half in range(2):
                    for kx in range(3):
                        at = 2 * kx * NB + half * CH
                        last = pe.matmul(cv_ps[:, half, 0:CH], diag[:, c, kx, :],
                                         relu_rows[:, yy % R_SLOTS, c, at:at + CH], start=kx == 0, stop=kx == 2)
                last.then_inc(centre_ready, 1)

            def to_tokens(h, z, zz, i):
                if i == 0:
                    pe.wait_ge(nsum_ready, h * H + z + 1)
                pe.wait_ge(gn_copied, 1 + h * (4 * H) + (4 * z + i - 1 if zz or i else 0))
                for t in range(2 * i, min(2 * i + 2, T)):
                    bank = 4 + 2 * (i % 2) + t % 2
                    pe.matmul(psum[:, bank, 0:C], pick[:, :], bias_rows[:, 0:C], start=True, stop=False)
                    for c in range(CK):
                        pe.matmul(psum[:, bank, 0:C], dw_rows[:, zz % D_SLOTS, c, NB + P * t:NB + P * (t + 1)],
                                  pw[:, c, :], start=False, stop=c == CK - 1)
                    for c in range(CK):
                        last = pe.transpose(psum[:, bank, C + P * c:C + P * (c + 1)],
                                            nsum[:, zz % N_SLOTS, c, P * t:P * (t + 1)], ident[:, :])
                last.then_inc(gn_ready, 1)

            def step(h, k, kk):
                y, yy, z, zz = k - 3, kk - 3, k - 6, kk - 6
                for c in range(CK):
                    if 0 <= yy < H and c == 0:
                        centre_taps(h, y, yy, 0)
                    if kk < H:
                        transpose_row(h, k, kk, c)
                    if 0 <= yy < H and c == 0:
                        centre_taps(h, y, yy, 1)
                    if 0 <= zz < H:
                        to_tokens(h, z, zz, 2 * c)
                        to_tokens(h, z, zz, 2 * c + 1)

            row_steps(pe, step)

            def transpose_tile(c, cc, it, n):
                slot = cc % TILE_SLOTS
                pe.wait_ge(tile_in[slot], 16 * Q * (times(cc, it, n, TILE_SLOTS) + 1))
                pe.wait_ge(lo_ready, c + 1)
                for k in range(4):
                    last = pe.transpose(psum[:, cc % 4, P * k:P * (k + 1)], x_tile[:, slot, P * k:P * (k + 1)], ident[:, :])
                last.then_inc(u_ready, 1)

            def hidden(c, cc):
                pe.wait_ge(lo_ready, 4 + c + 1)
                pe.wait_ge(pres_ready, c + 1)
                bank = psum[:, 4 + cc % 4, :]
                pe.matmul(bank, pick[:, :], bias_rows[:, C:C + HID], start=True, stop=False)
                for k in range(2 * CK):
                    hi = u_hi[:, cc % U_SLOTS, P * k:P * (k + 1)]
                    lo = u_lo[:, cc % U_SLOTS, P * k:P * (k + 1)]
                    pe.matmul(bank, hi, w1_hi[:, k, :], start=False, stop=False)
                    pe.matmul(bank, hi, w1_lo[:, k, :], start=False, stop=False)
                    last = pe.matmul(bank, lo, w1_hi[:, k, :], start=False, stop=k == 2 * CK - 1)
                last.then_inc(pre_ready, 1)

            def tile(c, cc, it, level, n, *_):
                if not isinstance(c, int) or c + AHEAD < TILES:
                    transpose_tile(c + AHEAD, cc + AHEAD, it, n)
                hidden(c, cc)

            for c in range(AHEAD):
                transpose_tile(c, c, 0, 0)
            tile(0, 0, 0, 0, 0)
            levels(pe, tile)


SETUP_DIAG = 1 + 6 + CK + 3 + 1 + CK + 3
SETUP_CST = SETUP_DIAG + 3 * CK + 1
SETUP_T = SETUP_CST + 4
SETUP_V = SETUP_T + 4 * CK + 1 + 2 + (1 + 6) + (1 + 3) + 1


def half_ops(steps=LAST_STEP + 1):
    n = 0
    for k in range(steps):
        if 0 <= k - 3 < H:
            n += CK * 3 * sum(0 <= k - 3 + d < H for d in (-2, 2))
        if 0 <= k - 5 < H:
            n += 1 + sum(0 <= k - 5 + d < H for d in (-1, 1))
    return n


_INPUTS = ["x", "L0_conv_dw_kernel", "L0_conv_dw_bias", "L0_conv_pw_kernel", "L0_conv_pw_bias",
           "L0_conv_gamma", "L0_conv_beta", "L0_conv_moving_mean", "L0_conv_moving_var",
           "L1_conv_w1", "L1_conv_b1", "L1_conv_w2", "L1_conv_b2", "L1_conv_w_y"]


def kernel(**inputs):
    import concourse.bacc as bacc
    from concourse.bass_utils import run_bass_kernel_spmd

    nc = bacc.Bacc("TRN2", target_bir_lowering=False, num_devices=1)
    arrays, aps = {}, []
    named = [(n, np.ascontiguousarray(inputs[n])) for n in _INPUTS]
    named = [(n, a.reshape(1) if a.ndim == 0 else a) for n, a in named]
    named += list(zip(("load_row", "store_row", "coef", "wrap", "side"), shape_tables()))
    for n, a in named:
        arrays[n] = a
        aps.append(nc.dram_tensor(n, a.shape, mybir.dt.from_np(a.dtype), kind="ExternalInput").ap())
    scratch = nc.dram_tensor("scratch", (H, WI, B, T, 2 * C), mybir.dt.float32, kind="Internal").ap()
    out = nc.dram_tensor("out", (B, H, W, C), mybir.dt.float32, kind="ExternalOutput").ap()
    build(nc, *aps, scratch, out)
    r = run_bass_kernel_spmd(nc, [arrays], core_ids=[0])
    return r.results[0]["out"]
```

```python
import numpy as np
from contextlib import ExitStack

import concourse.bass as bass
from concourse import mybir

B, H, W, C = 32, 56, 56, 256
HID = 512
P = 128
CK = C // P
NB = 16
HALVES = B // NB
WI = P // NB
T = W // WI
COLS = W * NB
PADX = 2
RROW = (W + 2 * PADX) * NB
DROW = (W + 2) * NB
R_SLOTS, D_SLOTS, X_SLOTS, O_SLOTS = 8, 4, 2, 2
UNROLL = 8
ROWS = HALVES * H
CENTRE_LAG, CONV_LAG, OUT_LAG = 2, 3, 5
EPS = 1e-3

RINGS = H // 2
Q = P // B
GROUPS = RINGS // Q
LEVELS = 8 * RINGS
STAGE_LEVELS = LEVELS // GROUPS
BODY_LEVELS = 8
U_SLOTS, TILE_SLOTS, OUT_SLOTS, AHEAD = 4, 8, 4, 2
TILES = 1 + sum(STAGE_LEVELS * (GROUPS - s) for s in range(GROUPS))
WRAP_LEVEL = 6
WIN = 13
PAD = 7
HIST = PAD + LEVELS + 1
OUT_OF_RANGE = B * H * W


def ring_point(r, i):
    if i < 0 or i >= max(1, 8 * r):
        return None
    if r == 0:
        return H // 2, W // 2
    e, k = divmod(i, 2 * r)
    y, x = ((-r, -r + k), (-r + k, r), (r, r - k), (r - k, -r))[e]
    y, x = y + H // 2, x + W // 2
    return (y, x) if 0 <= y < H and 0 <= x < W else None


def tile_sequence():
    seq = [(0, GROUPS)]
    for s in range(GROUPS):
        for level in range(STAGE_LEVELS * s, STAGE_LEVELS * (s + 1)):
            seq += [(level, g) for g in range(GROUPS - 1 - s, -1, -1)]
    return seq


def shape_tables():
    where = {ring_point(r, i): (r, i) for r in range(RINGS + 1) for i in range(max(1, 8 * r))
             if ring_point(r, i) is not None}
    assert len(where) == H * W
    load_row = np.zeros((1, TILES * Q), np.int32)
    store_row = np.full((P, TILES), OUT_OF_RANGE, np.int32)
    coef = np.zeros((P, TILES * WIN), np.float32)
    wrap = np.zeros((P, LEVELS // BODY_LEVELS), np.float32)
    img = np.arange(B)
    for c, (level, g) in enumerate(tile_sequence()):
        for q in range(Q):
            r = RINGS - Q + 1 - Q * g + q
            rows = slice(B * q, B * (q + 1))
            at = ring_point(r, level) if r >= 0 else None
            if at is not None:
                load_row[0, c * Q + q] = ((at[0] * WI + at[1] % WI) * B) * T + at[1] // WI
                store_row[rows, c] = (img * H + at[0]) * W + at[1]
            t = level + 1
            at = ring_point(r, t) if r >= 1 and g < GROUPS else None
            if at is None:
                continue
            y, x = at
            near = [where[p] for p in ((y - 1, x), (y + 1, x), (y, x - 1), (y, x + 1)) if p in where]
            before = [p for p in near if p < (r, t)]
            for r2, i2 in before:
                if t == 8 * r - 1 and i2 == 0:
                    assert before.count((r, 0)) == 1 and before.count((r - 1, 0)) == 1
                    assert level % BODY_LEVELS == WRAP_LEVEL and g == GROUPS - 1 - level // STAGE_LEVELS
                    wrap[rows, level // BODY_LEVELS] = 1.0 / len(near)
                    continue
                d = t - i2
                assert (r2 == r and d == 1) or (r2 == r - 1 and 1 <= d <= 7)
                col = WIN - 2 if r2 == r else WIN - 1 - 2 * (d - 1)
                n = GROUPS - level // STAGE_LEVELS
                coef[rows, (c - n + 1 + 2 * g) * WIN + col] = 1.0 / len(near)
    side = np.zeros((P, 4), np.float32)
    wi = np.arange(P) // NB
    for j, (edge, inner) in enumerate(((0, 4), (WI - 1, 4), (0, 3), (WI - 1, 3))):
        side[:, j] = 1.0 / np.where(wi == edge, inner - 1, inner)
    return load_row, store_row, coef, wrap, side


def build(nc, x, dwk, dwb, pwk, pwb, gamma, beta, mmean, mvar, w1, b1, w2, b2, wy,
          load_row, store_row, coef, wrap, side, scratch, out):
    f32, f32r = mybir.dt.float32, mybir.dt.float32r
    bf16, i32 = mybir.dt.bfloat16, mybir.dt.int32
    ALU = mybir.AluOpType
    ACT = mybir.ActivationFunctionType
    AX = mybir.AxisListType
    ctx = ExitStack()
    with ctx:
        def sb(name, shape, dt=f32):
            return ctx.enter_context(nc.sbuf_tensor(name, shape, dt))

        def sem(name):
            return ctx.enter_context(nc.semaphore(name))

        x_tok = sb("x_tok", [P, X_SLOTS, T * C])
        relu_rows = sb("relu_rows", [P, R_SLOTS, CK, RROW])
        dw_rows = sb("dw_rows", [P, D_SLOTS, CK, DROW])
        gn_out = sb("gn_out", [P, O_SLOTS, T, 2 * C])
        ident = sb("ident", [P, P])
        pw = sb("pw", [P, CK, C])
        taps = sb("taps", [P, CK, 9])
        w1_hi = sb("w1_hi", [P, 2 * CK, HID], f32r)
        w1_lo = sb("w1_lo", [P, 2 * CK, HID], f32r)
        u_hi = sb("u_hi", [P, U_SLOTS, 2 * C], f32r)
        u_lo = sb("u_lo", [P, U_SLOTS, 2 * C], f32r)
        v_row = sb("v_row", [P, HID])
        w2_row = sb("w2_row", [P, HID])
        wy_row = sb("wy_row", [P, C])
        b2_col = sb("b2_col", [P, 1])
        side_sb = sb("side_sb", [P, 4])
        bias_tmp = sb("bias_tmp", [P, 2, C + HID])
        bias_rows = sb("bias_rows", [P, C + HID], bf16)
        pick = sb("pick", [P, P], bf16)
        store_idx = sb("store_idx", [P, TILES], i32)
        s_col = sb("s_col", [P, GROUPS])
        y_lvl = sb("y_lvl", [P, 2, GROUPS])
        wrap_tmp = sb("wrap_tmp", [P, 1])
        win_tmp = sb("win_tmp", [P, GROUPS, WIN])
        wrap_sb = sb("wrap_sb", [P, LEVELS // BODY_LEVELS])
        idx_col = sb("idx_col", [P, OUT_SLOTS], i32)
        rr = relu_rows[:, :, :, :].rearrange("p a b c -> p (a b c)")
        coef_sb = rr[:, 0:TILES * WIN]
        hist = rr[:, TILES * WIN:TILES * WIN + GROUPS * HIST * 2].rearrange("p (g n) -> p g n", g=GROUPS)
        assert TILES * WIN + GROUPS * HIST * 2 <= R_SLOTS * CK * RROW
        dd = dw_rows[:, :, :, :].rearrange("p a b c -> p (a b c)")
        row_sb = dd[0:1, 0:TILES * Q].bitcast(i32)
        oo = gn_out[:, :, :, :].rearrange("p a b c -> p (a b c)")

        def part(n, k, size):
            at = part.at
            part.at += k * size
            return oo[:, at:at + k * size].rearrange("p (k n) -> p k n", k=k)
        part.at = 0
        x_tile = part("x_tile", TILE_SLOTS, 2 * C)
        pre_s = part("pre_s", 2, HID)
        th = part("th", 2, HID)
        o_tile = part("o_tile", OUT_SLOTS, C)
        prod = bias_tmp[:, 0, 0:HID]
        assert part.at <= O_SLOTS * T * 2 * C
        su = gn_out[:, :, :, :].rearrange("p a b c -> p (a b c)")
        gam, bet, mme, mva, pwb_r, inv, cst, t0, t1 = (su[:, C * i:C * (i + 1)] for i in range(9))
        o = 9 * C
        w1b = su[:, o:o + CK * HID].rearrange("p (k n) -> p k n", k=CK); o += CK * HID
        pw_t = su[:, o:o + CK * C].rearrange("p (k n) -> p k n", k=CK); o += CK * C
        dwb_b = su[:, o:o + CK * P].rearrange("p (k n) -> p k n", k=CK); o += CK * P
        cst_b = su[:, o:o + CK * P].rearrange("p (k n) -> p k n", k=CK); o += CK * P
        wy_b = su[:, o:o + CK * P].rearrange("p (k n) -> p k n", k=CK); o += CK * P
        b1_r = su[:, o:o + HID]; o += HID
        dwb_c = su[:, o:o + CK]; o += CK
        w1a = su[:, o:o + CK * HID].rearrange("p (k n) -> p k n", k=CK); o += CK * HID
        brow = bias_tmp[:, 0, :]
        brow2 = bias_tmp[:, 1, :]
        assert o <= O_SLOTS * T * 2 * C

        psum = ctx.enter_context(nc.psum_tensor("psum", [P, 8, 512], f32))
        x_ps = psum[:, 0:2 * CK, :].rearrange("p (c a) n -> p c (a n)", c=CK)

        x_in = [sem(f"x_in{i}") for i in range(X_SLOTS)]
        wts_in = sem("wts_in")
        setup_pe, setup_v, setup_a, setup_p = sem("setup_pe"), sem("setup_v"), sem("setup_a"), sem("setup_p")
        x_transposed = sem("x_transposed")
        row_ready = sem("row_ready")
        centre_ready = sem("centre_ready")
        conv_step = sem("conv_step")
        dw_ready = sem("dw_ready")
        gn_ready = sem("gn_ready")
        gn_copied = sem("gn_copied")
        stored = [sem(f"stored{i}") for i in range(O_SLOTS)]
        tabs_in = sem("tabs_in")
        hist_zero = sem("hist_zero")
        tile_in = [sem(f"tile_in{i}") for i in range(TILE_SLOTS)]
        u_ready = sem("u_ready")
        hi_ready = sem("hi_ready")
        lo_ready = sem("lo_ready")
        pre_ready = sem("pre_ready")
        pres_ready = sem("pres_ready")
        th_ready = sem("th_ready")
        y_ready = sem("y_ready")
        hist_ready = sem("hist_ready")
        win_ready = sem("win_ready")
        s_ready = sem("s_ready")
        wrap_step = sem("wrap_step")
        out_ready = sem("out_ready")
        idx_ready = sem("idx_ready")
        out_stored = sem("out_stored")
        pool_gate = sem("pool_gate")
        tile_out = [sem(f"tile_out{i}") for i in range(OUT_SLOTS)]

        x_v = x.rearrange("b h (w t) c -> h b w (t c)", t=T)
        sc_rows = scratch.rearrange("h w b t n -> (h w b t) n")
        sc_v = scratch.rearrange("h w (b a) t n -> h (w b) a (t n)", a=HALVES)
        out_rows = out.rearrange("b h w c -> (b h w) c")

        N_W = 17

        def row_steps(eng, step, last, start=lambda h, j: None):
            for h in range(HALVES):
                start(h, 0)
                for k in range(h * H, h * H + UNROLL):
                    step(k, k)
                with eng.Fori(1, H // UNROLL) as j:
                    start(h, j)
                    for kk in range(h * H + UNROLL, h * H + 2 * UNROLL):
                        step(j * UNROLL + (kk - UNROLL), kk)
            start(HALVES, 0)
            for k in range(ROWS, last + 1):
                step(k, k)

        def levels(eng, tile):
            c0 = 1
            for s in range(GROUPS):
                n = GROUPS - s
                iters = STAGE_LEVELS // BODY_LEVELS

                def body(it):
                    for l in range(BODY_LEVELS):
                        for j in range(n):
                            cc = c0 + l * n + j
                            tile(cc + it * (BODY_LEVELS * n), cc, it,
                                 s * STAGE_LEVELS + it * BODY_LEVELS + l, n, j, l, s * iters + it)

                last_stage = s == GROUPS - 1
                with eng.Fori(0, iters - last_stage) as it:
                    body(it)
                if last_stage:
                    body(iters - 1)
                c0 += STAGE_LEVELS * n

        def times(cc, it, n, slots):
            return cc // slots + it * (BODY_LEVELS * n // slots)

        block = ctx.enter_context(nc.Block())

        @block.sync
        def _(sp):
            bc = lambda a, n: a.partition_broadcast(P)
            loads = [
                (gam, bc(gamma, C)), (bet, bc(beta, C)), (mme, bc(mmean, C)), (mva, bc(mvar, C)),
                (pwb_r, bc(pwb, C)), (wy_row[:, :], bc(wy, C)), (w2_row[:, :], bc(w2, HID)),
                (b1_r, bc(b1, HID)), (b2_col[:, :], bc(b2, 1)),
                (pw[:, :, :], pwk.rearrange("a b (k p) n -> p (a b k) n", p=P)),
                (w1a, w1[0:C, :].rearrange("(k p) n -> p k n", p=P)),
                (w1b, w1[C:2 * C, :].rearrange("(k p) n -> p k n", p=P)),
                (side_sb[:, :], side), (store_idx[:, :], store_row), (wrap_sb[:, :], wrap),
            ]
            for dst, src in loads:
                sp.dma_start(dst, src).then_inc(wts_in, 16)
            for k in range(CK):
                sp.dma_start(taps[:, k, :], dwk.rearrange("a b o (k p) -> k p (a b o)", p=P)[k],
                             allow_slow_non_contiguous=True).then_inc(wts_in, 16)
            sp.dma_start(dwb_c, dwb.rearrange("(k p) -> p k", p=P),
                         allow_slow_non_contiguous=True).then_inc(wts_in, 16)

            def step(k, kk):
                if kk < ROWS:
                    if kk >= X_SLOTS:
                        sp.wait_ge(x_transposed, CK * k - CK * (X_SLOTS - 1))
                    sp.dma_start(x_tok[:, kk % X_SLOTS, :],
                                 x_v[k - kk // H * H, kk // H:B:HALVES, :, :]).then_inc(x_in[kk % X_SLOTS], 16)
                z, zz = k - (OUT_LAG + 2), kk - (OUT_LAG + 2)
                if zz >= 0:
                    sp.wait_ge(gn_copied, 4 * z + 4)
                    sp.dma_start(sc_v[z - zz // H * H, :, zz // H, :],
                                 gn_out[:, zz % O_SLOTS, :, :].rearrange("p t n -> p (t n)")
                                 ).then_inc(stored[zz % O_SLOTS], 16)

            row_steps(sp, step, ROWS - 1 + OUT_LAG + 2)

            for i in range(O_SLOTS):
                sp.wait_ge(stored[i], 16 * (ROWS // O_SLOTS))
            sp.dma_start(row_sb, load_row).then_inc(tabs_in, 16)
            sp.dma_start(coef_sb, coef).then_inc(tabs_in, 16)
            sp.wait_ge(tabs_in, 32)
            regs = [sp.alloc_register(f"row{q}") for q in range(Q)]

            def load(c, cc, *_):
                sp.load(regs, row_sb[0:1, bass.ds(c * Q, Q)])
                sp.wait_ge(out_ready, c + 1)
                for q in range(Q):
                    row = sp.snap(regs[q], min_val=0, max_val=(H * WI - 1) * B * T + T - 1)
                    sp.dma_start(x_tile[B * q:B * (q + 1), cc % TILE_SLOTS, :],
                                 sc_rows[bass.ds(row, B, T), :]).then_inc(tile_in[cc % TILE_SLOTS], 16)

            load(0, 0)
            levels(sp, load)

        @block.gpsimd
        def _(pool):
            pool.sem_inc(out_stored, OUT_SLOTS)
            pool.memset(ident[:, :], 0.0).then_inc(setup_p, 1)
            pool.memset(pick[:, :], 0.0)
            pool.memset(bias_rows[:, :], 0.0)
            pool.memset(relu_rows[:, :, :, :], 0.0)
            pool.memset(dw_rows[:, :, :, :], 0.0)
            pool.memset(s_col[:, :], 0.0).then_inc(setup_p, 1)
            pool.wait_ge(setup_p, 2)
            pool.affine_select(out=ident[:, :], in_=ident[:, :], compare_op=ALU.not_equal, fill=1.0,
                               base=0, pattern=[[-1, P]], channel_multiplier=1).then_inc(setup_p, 1)
            for i in range(O_SLOTS):
                pool.wait_ge(stored[i], 16 * (ROWS // O_SLOTS))
            pool.memset(hist, 0.0).then_inc(hist_zero, 1)
            pool.wait_ge(wts_in, 16 * (N_W + 1))

            def store(c, cc, it, level, n, *_):
                slot = cc % OUT_SLOTS
                pool.wait_ge(out_stored, c + 1)
                pool.sem_inc(pool_gate, 1)
                pool.tensor_copy(idx_col[:, slot:slot + 1], store_idx[:, bass.ds(c, 1)]).then_inc(idx_ready, 1)
                pool.wait_ge(idx_ready, c + 1)
                pool.sem_inc(pool_gate, 1)
                pool.wait_ge(out_ready, TILE_SLOTS + c + 1)
                pool.sem_inc(pool_gate, 1)
                pool.indirect_dma_start(out_rows, bass.IndirectOffsetOnAxis(idx_col[:, slot:slot + 1], 0),
                                        o_tile[:, slot, :], None, bounds_check=OUT_OF_RANGE - 1,
                                        oob_is_err=False).then_inc(tile_out[slot], 16)
                if cc:
                    pool.wait_ge(tile_out[(cc - 1) % OUT_SLOTS], 16 * (times(cc - 1, it, n, OUT_SLOTS) + 1))
                    pool.sem_inc(out_stored, 1)

            store(0, 0, 0, 0, 0)
            levels(pool, store)
            for i in range(OUT_SLOTS):
                pool.wait_ge(tile_out[i], 16 * len(range(i, TILES, OUT_SLOTS)))

        @block.scalar
        def _(act):
            act.wait_ge(setup_v, 1)
            act.activation(t1, t0, ACT.Sqrt).then_inc(setup_a, 1)
            act.sem_inc(th_ready, 2)
            act.wait_ge(setup_p, 3)
            act.wait_ge(setup_pe, 7)
            act.wait_ge(setup_v, SETUP_V)

            def relu(k, kk, c):
                act.wait_ge(x_transposed, CK * k + c + 1)
                if c == 0 and kk >= R_SLOTS:
                    act.wait_ge(dw_ready, k - 5)
                act.activation(relu_rows[:, kk % R_SLOTS, c, PADX * NB:PADX * NB + COLS].rearrange(
                                   "p (w t b) -> p t b w", t=T, b=NB),
                               x_ps[:, c, 0:COLS].rearrange("p (t b w) -> p t b w", b=NB, w=WI),
                               ACT.Relu).then_inc(row_ready, 1)

            def centre_tap(y, yy, c):
                act.wait_ge(row_ready, CK * y + c + 1)
                if c == 0 and yy >= D_SLOTS:
                    act.wait_ge(gn_ready, 4 * y - 8)
                act.activation(dw_rows[:, yy % D_SLOTS, c, NB:NB + COLS],
                               relu_rows[:, yy % R_SLOTS, c, PADX * NB:PADX * NB + COLS], ACT.Copy,
                               scale=taps[:, c, 4:5]).then_inc(centre_ready, 1)

            def copy_out(z, zz, i):
                edge = zz % H in (0, H - 1)
                tiles = range(2 * i, min(2 * i + 2, T))
                act.wait_ge(gn_ready, 4 * z + i + 1)
                if i == 0 and zz >= O_SLOTS:
                    act.wait_ge(stored[zz % O_SLOTS], 8 * (z - zz % O_SLOTS))
                bank = 4 + 2 * (i % 2)
                act.activation(gn_out[:, zz % O_SLOTS, tiles[0]:tiles[-1] + 1, 0:C],
                               psum[:, bank:bank + len(tiles), 0:C], ACT.Copy)
                inner = [t for t in tiles if t not in (0, T - 1)]
                for t in tiles:
                    if t in (0, T - 1):
                        col = (2 if edge else 0) + (t == T - 1)
                        last = act.activation(gn_out[:, zz % O_SLOTS, t, C:2 * C],
                                              psum[:, bank + t % 2, C:2 * C], ACT.Copy,
                                              scale=side_sb[:, col:col + 1])
                if inner:
                    b0 = bank + inner[0] % 2
                    last = act.activation(gn_out[:, zz % O_SLOTS, inner[0]:inner[-1] + 1, C:2 * C],
                                          psum[:, b0:b0 + len(inner), C:2 * C], ACT.Copy,
                                          scale=1.0 / (3 if edge else 4))
                last.then_inc(gn_copied, 1)

            def step(k, kk):
                for c in range(CK):
                    if kk < ROWS:
                        relu(k, kk, c)
                    if kk >= OUT_LAG:
                        copy_out(k - OUT_LAG, kk - OUT_LAG, 2 * c)
                        copy_out(k - OUT_LAG, kk - OUT_LAG, 2 * c + 1)
                if 0 <= kk - CENTRE_LAG < ROWS:
                    for c in range(CK):
                        centre_tap(k - CENTRE_LAG, kk - CENTRE_LAG, c)

            row_steps(act, step, ROWS - 1 + OUT_LAG)

            def high_part(c, cc):
                act.wait_ge(u_ready, c + 1)
                act.wait_ge(pre_ready, c + 1)
                act.activation(u_hi[:, cc % U_SLOTS, :], psum[:, cc % 4, :], ACT.Copy).then_inc(hi_ready, 1)

            def tile(c, cc, *_):
                if not isinstance(c, int) or c + AHEAD < TILES:
                    high_part(c + AHEAD, cc + AHEAD)
                act.wait_ge(pres_ready, 4 + c + 1)
                act.wait_ge(y_ready, c + 1)
                act.activation(th[:, cc % 2, :], pre_s[:, cc % 2, :], ACT.Tanh).then_inc(th_ready, 1)

            for c in range(AHEAD):
                high_part(c, c)
            tile(0, 0)
            levels(act, tile)

        @block.vector
        def _(dve):
            done = [0]

            def link(ins):
                done[0] += 1
                ins.then_inc(setup_v, 1)
                dve.wait_ge(setup_v, done[0])

            dve.wait_ge(wts_in, 16 * (N_W + 1))
            link(dve.tensor_scalar(t0, mva, EPS, None, ALU.add))
            dve.wait_ge(setup_a, 1)
            link(dve.reciprocal(inv, t1))
            link(dve.tensor_tensor(inv, inv, t0, ALU.mult))
            link(dve.tensor_tensor(t1, t1, inv, ALU.add))
            link(dve.tensor_scalar(t1, t1, 0.5, None, ALU.mult))
            link(dve.reciprocal(inv, t1))
            link(dve.tensor_tensor(inv, inv, gam, ALU.mult))
            for k in range(CK):
                link(dve.tensor_tensor(pw[:, k, :], pw[:, k, :], inv, ALU.mult))
            link(dve.tensor_tensor(cst, pwb_r, mme, ALU.subtract))
            link(dve.tensor_tensor(cst, cst, inv, ALU.mult))
            link(dve.tensor_tensor(cst, cst, bet, ALU.add))
            link(dve.memset(dwb_b, 0.0))
            for k in range(CK):
                link(dve.tensor_scalar(dwb_b[:, k, :], dwb_b[:, k, :], dwb_c[:, k:k + 1], None, ALU.add))
            dve.wait_ge(setup_p, 3)
            for p in (0, 32, 64):
                link(dve.memset(pick[p:p + 1, :], 1.0))
            dve.wait_ge(setup_pe, 1)
            link(dve.tensor_tensor(cst, cst, psum[:, 0, 0:C], ALU.add))
            assert done[0] == SETUP_CST
            dve.wait_ge(setup_pe, 2)
            link(dve.tensor_copy(pw_t[:, 0, :], psum[:, 1, 0:C]))
            link(dve.tensor_copy(pw_t[:, 1, :], psum[:, 1, C:2 * C]))
            link(dve.tensor_copy(cst_b, psum[:, 2, 0:C].rearrange("p (k n) -> p k n", k=CK)))
            link(dve.tensor_copy(wy_b, psum[:, 2, C:2 * C].rearrange("p (k n) -> p k n", k=CK)))
            assert done[0] == SETUP_T
            dve.wait_ge(setup_pe, 3)
            for k in range(2 * CK):
                w = w1a[:, k, :] if k < CK else psum[:, 2 + k, :]
                link(dve.tensor_copy(w1_hi[:, k, :], w))
                link(dve.tensor_tensor(w1_lo[:, k, :], w, w1_hi[:, k, :].bitcast(f32), ALU.subtract))
            dve.wait_ge(setup_pe, 4)
            link(dve.tensor_copy(v_row[:, :], psum[:, 6, :]))
            dve.wait_ge(setup_pe, 5)
            link(dve.tensor_copy(brow[:, 0:C], cst))
            link(dve.tensor_tensor(brow[:, C:C + HID], b1_r, psum[:, 7, :], ALU.add))
            for i, p in enumerate((0, 32, 64)):
                link(dve.tensor_copy(bias_rows[p:p + 1, :], brow[p:p + 1, :]))
                if i < 2:
                    for p2 in (0, 32, 64)[i + 1:]:
                        link(dve.tensor_copy(bias_rows[p2:p2 + 1, :], brow[p2:p2 + 1, :]))
                        link(dve.tensor_tensor(brow2[p2:p2 + 1, :], brow[p2:p2 + 1, :],
                                               bias_rows[p2:p2 + 1, :], ALU.subtract))
                        link(dve.tensor_copy(brow[p2:p2 + 1, :], brow2[p2:p2 + 1, :]))
            assert done[0] == SETUP_V
            dve.sem_inc(pres_ready, 4)
            dve.sem_inc(y_ready, 2)
            dve.sem_inc(s_ready, 1)
            dve.sem_inc(lo_ready, 4)
            dve.sem_inc(out_ready, TILE_SLOTS)

            ops = {"n": 0}

            def start(h, j):
                before = chained_ops(h * H)
                if isinstance(j, int):
                    ops["n"] = before
                else:
                    first = chained_ops(h * H + UNROLL)
                    body = chained_ops(h * H + 2 * UNROLL) - first
                    ops["n"] = (first - body) + j * body

            def conv_chain(y, yy, c):
                dst = dw_rows[:, yy % D_SLOTS, c, NB:NB + COLS]
                steps = []
                for ky, kx in CONV_TAPS:
                    if 0 <= yy % H + 2 * (ky - 1) < H:
                        src = relu_rows[:, (yy + 2 * (ky - 1)) % R_SLOTS, c, 2 * kx * NB:2 * kx * NB + COLS]
                        steps.append((src, taps[:, c, 3 * ky + kx:3 * ky + kx + 1]))
                for i, (src, w) in enumerate(steps):
                    if i == 0:
                        dve.wait_ge(centre_ready, CK * y + c + 1)
                    ins = dve.scalar_tensor_tensor(out=dst, in0=src, scalar=w, in1=dst, op0=ALU.mult, op1=ALU.add)
                    ins.then_inc(conv_step, 1)
                    ops["n"] = ops["n"] + 1
                    n = ops["n"]
                    yield
                    dve.wait_ge(conv_step, n)

            def step(k, kk):
                y, yy = k - CONV_LAG, kk - CONV_LAG
                if not 0 <= yy < ROWS:
                    return
                if yy % H + 2 < H:
                    dve.wait_ge(row_ready, CK * y + 3 * CK)
                else:
                    dve.wait_ge(row_ready, CK * H * (yy // H + 1))
                chains = [conv_chain(y, yy, c) for c in range(CK)]
                while chains:
                    for chain in list(chains):
                        if next(chain, chain) is chain:
                            chains.remove(chain)
                dve.sem_inc(dw_ready, 1)

            row_steps(dve, step, ROWS - 1 + CONV_LAG, start)

            dve.wait_ge(tabs_in, 32)
            dve.wait_ge(hist_zero, 1)

            def low_part(c, cc):
                dve.wait_ge(hi_ready, c + 1)
                slot = cc % U_SLOTS
                dve.tensor_tensor(u_lo[:, slot, :], psum[:, cc % 4, :], u_hi[:, slot, :].bitcast(f32),
                                  ALU.subtract).then_inc(lo_ready, 1)

            def add_s(c, cc, level, g):
                dve.wait_ge(pre_ready, 4 + c + 1)
                dve.wait_ge(th_ready, c + 1)
                dve.wait_ge(s_ready, level + 1)
                dve.scalar_tensor_tensor(out=pre_s[:, cc % 2, :], in0=v_row[:, :], scalar=s_col[:, g:g + 1],
                                         in1=psum[:, 4 + cc % 4, :], op0=ALU.mult,
                                         op1=ALU.add).then_inc(pres_ready, 1)

            def dot(c, cc, y):
                dve.wait_ge(th_ready, 2 + c + 1)
                dve.tensor_tensor_reduce(out=prod, in0=th[:, cc % 2, :], in1=w2_row[:, :], scale=1.0,
                                         scalar=b2_col[:, 0:1], op0=ALU.mult, op1=ALU.add,
                                         accum_out=y).then_inc(y_ready, 1)

            def finish(c, cc, y):
                dve.wait_ge(y_ready, 2 + c + 1)
                dve.wait_ge(out_stored, c + 1)
                dve.scalar_tensor_tensor(out=o_tile[:, cc % OUT_SLOTS, :], in0=wy_row[:, :], scalar=y,
                                         in1=x_tile[:, cc % TILE_SLOTS, 0:C], op0=ALU.mult,
                                         op1=ALU.add).then_inc(out_ready, 1)

            def next_s(c, level, n, l, body, ys):
                dve.wait_ge(y_ready, 2 + c + 1)
                own = (level + PAD) * 2
                dve.tensor_copy(hist[:, 0:n, bass.ds(own, 1)], ys[:, 0:n].rearrange("p (g o) -> p g o", o=1))
                for q in range(Q):
                    src = ys[B * ((q - 1) % Q):B * ((q - 1) % Q + 1), (q == 0):n]
                    if q or n > 1:
                        last = dve.tensor_copy(hist[B * q:B * (q + 1), 0:n - (q == 0), bass.ds(own + 1, 1)],
                                               src.rearrange("p (g o) -> p g o", o=1))
                last.then_inc(hist_ready, 1)
                dve.wait_ge(hist_ready, level + 2)
                first = c - (n - 1)
                dve.tensor_tensor(win_tmp[:, 0:n, :], hist[:, 0:n, bass.ds(level * 2 + 3, WIN)],
                                  coef_sb[:, bass.ds(first * WIN, n * WIN)].rearrange("p (g w) -> p g w", g=n),
                                  ALU.mult).then_inc(win_ready, 1)
                dve.wait_ge(win_ready, level + 1)
                dve.tensor_reduce(s_col[:, 0:n], win_tmp[:, 0:n, :], axis=AX.X, op=ALU.add).then_inc(s_ready, 1)
                if l == WRAP_LEVEL:
                    g = n - 1
                    dve.tensor_tensor(wrap_tmp[:, :], hist[:, g, 2 * PAD:2 * PAD + 1],
                                      hist[:, g, 2 * PAD + 1:2 * PAD + 2], ALU.add).then_inc(wrap_step, 1)
                    dve.wait_ge(s_ready, level + 2)
                    dve.wait_ge(wrap_step, 2 * body + 1)
                    dve.scalar_tensor_tensor(out=s_col[:, g:g + 1], in0=wrap_tmp[:, :],
                                             scalar=wrap_sb[:, bass.ds(body, 1)], in1=s_col[:, g:g + 1],
                                             op0=ALU.mult, op1=ALU.add).then_inc(wrap_step, 1)
                    dve.wait_ge(wrap_step, 2 * body + 2)

            def y_of(level, g):
                return y_lvl[:, level % 2, g:g + 1]

            for c in range(AHEAD):
                low_part(c, c)
            centre_y = y_of(1, 0)
            add_s(0, 0, 0, 0)
            low_part(AHEAD, AHEAD)
            dot(0, 0, centre_y)
            dve.wait_ge(y_ready, 2 + 1)
            dve.tensor_copy(hist[0:B, GROUPS - 1, 2 * PAD + 1:2 * PAD + 2],
                            y_lvl[B * (Q - 1):P, 1, 0:1]).then_inc(hist_ready, 1)

            def tile(c, cc, it, level, n, j, l, body):
                g = n - 1 - j
                add_s(c, cc, level, g)
                if not isinstance(c, int) or c + AHEAD < TILES:
                    low_part(c + AHEAD, cc + AHEAD)
                if j:
                    dot(c - 1, cc - 1, y_of(l, g + 1))
                finish(c - 1, cc - 1, y_of(l, g + 1) if j else y_of(l - 1, 0))
                if j == n - 1:
                    dot(c, cc, y_of(l, 0))
                    next_s(c, level, n, l, body, y_lvl[:, l % 2, 0:GROUPS])

            levels(dve, tile)
            finish(TILES - 1, TILES - 1, y_of(BODY_LEVELS - 1, 0))

        @block.tensor
        def _(pe):
            pe.wait_ge(setup_v, SETUP_PICK)
            for k in range(CK):
                last = pe.matmul(psum[:, 0, 0:C], dwb_b[:, k, :], pw[:, k, :], start=k == 0, stop=k == CK - 1)
            last.then_inc(setup_pe, 1)
            pe.wait_ge(setup_v, SETUP_CST)
            for k in range(CK):
                for m in range(CK):
                    pe.transpose(psum[:, 1, C * m + P * k:C * m + P * (k + 1)], pw[:, k, P * m:P * (m + 1)], ident[:, :])
            for k in range(CK):
                pe.transpose(psum[:, 2, P * k:P * (k + 1)], cst[:, P * k:P * (k + 1)], ident[:, :])
                last = pe.transpose(psum[:, 2, C + P * k:C + P * (k + 1)], wy_row[:, P * k:P * (k + 1)], ident[:, :])
            last.then_inc(setup_pe, 1)
            pe.wait_ge(setup_v, SETUP_T)
            for k in range(CK):
                for m in range(CK):
                    last = pe.matmul(psum[:, 4 + k, :], pw_t[:, m, P * k:P * (k + 1)], w1b[:, m, :],
                                     start=m == 0, stop=m == CK - 1)
            last.then_inc(setup_pe, 1)
            for bank, lhs in ((6, wy_b), (7, cst_b)):
                for m in range(CK):
                    last = pe.matmul(psum[:, bank, :], lhs[:, m, :], w1b[:, m, :], start=m == 0, stop=m == CK - 1)
                last.then_inc(setup_pe, 1)
            pe.wait_ge(setup_v, SETUP_V)
            pe.sem_inc(setup_pe, 2)
            pe.sem_inc(pre_ready, 4)

            def transpose_row(k, kk, c):
                if c == 0:
                    pe.wait_ge(x_in[kk % X_SLOTS], 8 * (k - kk % X_SLOTS) + 16)
                if kk:
                    pe.wait_ge(row_ready, CK * k + c + 1 - CK)
                for t in range(T):
                    last = pe.transpose(x_ps[:, c, P * t:P * (t + 1)],
                                        x_tok[:, kk % X_SLOTS, t * C + c * P:t * C + (c + 1) * P], ident[:, :])
                last.then_inc(x_transposed, 1)

            def to_tokens(z, zz, i):
                if i == 0:
                    pe.wait_ge(dw_ready, z + (2 if zz % H < H - 1 else 1))
                if 4 * zz + i >= 2:
                    pe.wait_ge(gn_copied, 4 * z + i - 1)
                for t in range(2 * i, min(2 * i + 2, T)):
                    bank = 4 + 2 * (i % 2) + t % 2
                    at = NB + P * t
                    pe.matmul(psum[:, bank, 0:C], pick[:, :], bias_rows[:, 0:C], start=True, stop=False)
                    for c in range(CK):
                        pe.matmul(psum[:, bank, 0:C], dw_rows[:, zz % D_SLOTS, c, at:at + P],
                                  pw[:, c, :], start=False, stop=c == CK - 1)
                    near = [(zz, at - NB), (zz, at + NB)]
                    near += [(zz + d, at) for d in (-1, 1) if 0 <= zz % H + d < H]
                    for c in range(CK):
                        for m, (row, col) in enumerate(near):
                            last = pe.matmul(psum[:, bank, C + P * c:C + P * (c + 1)],
                                             dw_rows[:, row % D_SLOTS, c, col:col + P], ident[:, :],
                                             start=m == 0, stop=m == len(near) - 1, is_transpose=True)
                last.then_inc(gn_ready, 1)

            def step(k, kk):
                for c in range(CK):
                    if kk < ROWS:
                        transpose_row(k, kk, c)
                    if kk >= OUT_LAG:
                        to_tokens(k - OUT_LAG, kk - OUT_LAG, 2 * c)
                        to_tokens(k - OUT_LAG, kk - OUT_LAG, 2 * c + 1)

            row_steps(pe, step, ROWS - 1 + OUT_LAG)

            def transpose_tile(c, cc, it, n):
                slot = cc % TILE_SLOTS
                pe.wait_ge(tile_in[slot], 16 * Q * (times(cc, it, n, TILE_SLOTS) + 1))
                pe.wait_ge(lo_ready, c + 1)
                for k in range(4):
                    last = pe.transpose(psum[:, cc % 4, P * k:P * (k + 1)], x_tile[:, slot, P * k:P * (k + 1)], ident[:, :])
                last.then_inc(u_ready, 1)

            def hidden(c, cc):
                pe.wait_ge(lo_ready, 4 + c + 1)
                pe.wait_ge(pres_ready, c + 1)
                bank = psum[:, 4 + cc % 4, :]
                pe.matmul(bank, pick[:, :], bias_rows[:, C:C + HID], start=True, stop=False)
                for k in range(2 * CK):
                    hi = u_hi[:, cc % U_SLOTS, P * k:P * (k + 1)]
                    lo = u_lo[:, cc % U_SLOTS, P * k:P * (k + 1)]
                    pe.matmul(bank, hi, w1_hi[:, k, :], start=False, stop=False)
                    pe.matmul(bank, hi, w1_lo[:, k, :], start=False, stop=False)
                    last = pe.matmul(bank, lo, w1_hi[:, k, :], start=False, stop=k == 2 * CK - 1)
                last.then_inc(pre_ready, 1)

            def tile(c, cc, it, level, n, *_):
                if not isinstance(c, int) or c + AHEAD < TILES:
                    transpose_tile(c + AHEAD, cc + AHEAD, it, n)
                hidden(c, cc)

            for c in range(AHEAD):
                transpose_tile(c, c, 0, 0)
            tile(0, 0, 0, 0, 0)
            levels(pe, tile)


SETUP_PICK = 1 + 6 + CK + 3 + 1 + CK + 3
SETUP_CST = SETUP_PICK + 1
SETUP_T = SETUP_CST + 4
SETUP_V = SETUP_T + 4 * CK + 1 + 2 + (1 + 6) + (1 + 3) + 1


CONV_TAPS = [(1, 0), (1, 2)] + [(ky, kx) for ky in (0, 2) for kx in range(3)]


def chained_ops(steps):
    return sum(CK * sum(0 <= y % H + 2 * (ky - 1) < H for ky, kx in CONV_TAPS)
               for y in range(steps - CONV_LAG))


_INPUTS = ["x", "L0_conv_dw_kernel", "L0_conv_dw_bias", "L0_conv_pw_kernel", "L0_conv_pw_bias",
           "L0_conv_gamma", "L0_conv_beta", "L0_conv_moving_mean", "L0_conv_moving_var",
           "L1_conv_w1", "L1_conv_b1", "L1_conv_w2", "L1_conv_b2", "L1_conv_w_y"]


def kernel(**inputs):
    import concourse.bacc as bacc
    from concourse.bass_utils import run_bass_kernel_spmd

    nc = bacc.Bacc("TRN2", target_bir_lowering=False, num_devices=1)
    arrays, aps = {}, []
    named = [(n, np.ascontiguousarray(inputs[n])) for n in _INPUTS]
    named = [(n, a.reshape(1) if a.ndim == 0 else a) for n, a in named]
    named += list(zip(("load_row", "store_row", "coef", "wrap", "side"), shape_tables()))
    for n, a in named:
        arrays[n] = a
        aps.append(nc.dram_tensor(n, a.shape, mybir.dt.from_np(a.dtype), kind="ExternalInput").ap())
    scratch = nc.dram_tensor("scratch", (H, WI, B, T, 2 * C), mybir.dt.float32, kind="Internal").ap()
    out = nc.dram_tensor("out", (B, H, W, C), mybir.dt.float32, kind="ExternalOutput").ap()
    build(nc, *aps, scratch, out)
    r = run_bass_kernel_spmd(nc, [arrays], core_ids=[0])
    return r.results[0]["out"]
```
